# Optimizing a Trainium2 kernel written in Bass

```python
import numpy as np
import jax
import jax.numpy as jnp

def _softmax(x, axis=-1):
    return jax.nn.softmax(x, axis=axis)

def _gelu(x):
    return jax.nn.gelu(x, approximate=True)

def _silu(x):
    return jax.nn.silu(x)

def _sigmoid(x):
    return jax.nn.sigmoid(x)

def _layernorm(x, axis=-1, eps=1e-05):
    m = jnp.mean(x, axis=axis, keepdims=True)
    v = jnp.var(x, axis=axis, keepdims=True)
    return (x - m) / jnp.sqrt(v + eps)

def _scatter_add(tgt, idx, src, axis=0):
    return tgt.at[idx].add(src)

def _segment_sum(src, seg, n):
    return jax.ops.segment_sum(src, seg, n)
kernel_name = 'mk_macaron_d1_jaxref_r8_72aaf0'

def setup_inputs(seed: int=0):
    np.random.seed(seed)
    _w = jnp.asarray

    def _L0_attn_setup():
        import jax, jax.numpy as jnp
        import numpy as np
        N_HEADS = 16
        ROPE_BASE = 10000.0

        def _rope(x):
            B, L, H, Dh = x.shape
            half = Dh // 2
            inv_freq = 1.0 / ROPE_BASE ** (jnp.arange(0, half, dtype=jnp.float32) / half)
            ang = jnp.arange(L, dtype=jnp.float32)[:, None] * inv_freq[None, :]
            cos = jnp.concatenate([jnp.cos(ang), jnp.cos(ang)], axis=-1).astype(x.dtype)
            sin = jnp.concatenate([jnp.sin(ang), jnp.sin(ang)], axis=-1).astype(x.dtype)
            cos = cos[None, :, None, :]
            sin = sin[None, :, None, :]
            x1, x2 = (x[..., :half], x[..., half:])
            rot = jnp.concatenate([-x2, x1], axis=-1)
            return x * cos + rot * sin
        key = jax.random.key(seed)
        k1, k2, k3 = jax.random.split(key, 3)
        B, L, D = (2, 256, 128)
        x = jax.random.normal(k1, (B, L, D), dtype=jnp.float32)
        w_qkv = jax.random.normal(k2, (3 * D, D), dtype=jnp.float32) * D ** (-0.5)
        w_out = jax.random.normal(k3, (D, D), dtype=jnp.float32) * D ** (-0.5)
        return {'x': x, 'w_qkv': w_qkv, 'w_out': w_out}
    _L0_attn_in = _L0_attn_setup()

    def _L0_ffn_setup():
        import jax, jax.numpy as jnp
        import numpy as np
        B, S, D, E, F = (2, 256, 128, 14, 256)
        key = jax.random.key(seed)
        k = jax.random.split(key, 4)
        h = jax.random.normal(k[0], (B, S, D), dtype=jnp.float32)
        router_w = jax.random.normal(k[1], (D, E), dtype=jnp.float32) * 0.02
        w1 = jax.random.uniform(k[2], (E, D, F), dtype=jnp.float32, minval=-1.0, maxval=1.0) * float(np.sqrt(6.0 / D))
        w2 = jax.random.uniform(k[3], (E, F, D), dtype=jnp.float32, minval=-1.0, maxval=1.0) * float(np.sqrt(6.0 / F))
        b1 = jnp.zeros((E, F), dtype=jnp.float32)
        b2 = jnp.zeros((E, D), dtype=jnp.float32)
        return {'h': h, 'router_w': router_w, 'w1': w1, 'b1': b1, 'w2': w2, 'b2': b2}
    _L0_ffn_in = _L0_ffn_setup()
    _d = {'L0_attn_x': _L0_attn_in['x'], 'L0_attn_w_qkv': _L0_attn_in['w_qkv'], 'L0_attn_w_out': _L0_attn_in['w_out'], 'L0_ffn_router_w': _L0_ffn_in['router_w'], 'L0_ffn_w1': _L0_ffn_in['w1'], 'L0_ffn_b1': _L0_ffn_in['b1'], 'L0_ffn_w2': _L0_ffn_in['w2'], 'L0_ffn_b2': _L0_ffn_in['b2']}
    _x0 = _d['L0_attn_x']
    _d['L0_attn_x'] = jax.random.normal(jax.random.fold_in(jax.random.key(seed), 1), (4, 1024, 128), dtype=_x0.dtype)
    del _x0
    return _d

def reference(L0_attn_x, L0_attn_w_qkv, L0_attn_w_out, L0_ffn_router_w, L0_ffn_w1, L0_ffn_b1, L0_ffn_w2, L0_ffn_b2):

    def _L0_attn_ref(x, w_qkv, w_out):
        import jax, jax.numpy as jnp
        import numpy as np
        N_HEADS = 16
        ROPE_BASE = 10000.0

        def _rope(x):
            B, L, H, Dh = x.shape
            half = Dh // 2
            inv_freq = 1.0 / ROPE_BASE ** (jnp.arange(0, half, dtype=jnp.float32) / half)
            ang = jnp.arange(L, dtype=jnp.float32)[:, None] * inv_freq[None, :]
            cos = jnp.concatenate([jnp.cos(ang), jnp.cos(ang)], axis=-1).astype(x.dtype)
            sin = jnp.concatenate([jnp.sin(ang), jnp.sin(ang)], axis=-1).astype(x.dtype)
            cos = cos[None, :, None, :]
            sin = sin[None, :, None, :]
            x1, x2 = (x[..., :half], x[..., half:])
            rot = jnp.concatenate([-x2, x1], axis=-1)
            return x * cos + rot * sin
        B, L, D = x.shape
        H = N_HEADS
        Dh = D // H
        qkv = jnp.einsum('bld,ed->ble', x, w_qkv)
        q, k, v = jnp.split(qkv, 3, axis=-1)
        q = q.reshape(B, L, H, Dh)
        k = k.reshape(B, L, H, Dh)
        v = v.reshape(B, L, H, Dh)
        q = _rope(q)
        k = _rope(k)
        scale = 1.0 / jnp.sqrt(jnp.asarray(Dh, dtype=x.dtype))
        scores = jnp.einsum('blhd,bmhd->bhlm', q, k) * scale
        attn = jax.nn.softmax(scores, axis=-1)
        out = jnp.einsum('bhlm,bmhd->blhd', attn, v).reshape(B, L, D)
        return jnp.einsum('bld,ed->ble', out, w_out)

    def _L0_ffn_ref(h, router_w, w1, b1, w2, b2):
        import jax, jax.numpy as jnp
        import numpy as np
        B, S, D, E, F = (2, 256, 128, 14, 256)
        Bb, Ss, Dd = h.shape
        x = h.reshape(-1, Dd)
        logits = x @ router_w
        assignments = jnp.argmax(logits, axis=-1)
        probs = jax.nn.softmax(logits, axis=-1)
        weights = jnp.take_along_axis(probs, assignments[:, None], axis=1)[:, 0]
        hid = jnp.einsum('nd,edf->nef', x, w1) + b1
        hid = jax.nn.gelu(hid, approximate=False)
        all_out = jnp.einsum('nef,efd->ned', hid, w2) + b2
        sel = jnp.take_along_axis(all_out, assignments[:, None, None], axis=1)[:, 0, :]
        moe_out = (sel * weights[:, None]).reshape(Bb, Ss, Dd)
        return moe_out
    x = L0_attn_x
    x = x + 0.5 * _L0_ffn_ref(_layernorm(x, axis=-1), L0_ffn_router_w, L0_ffn_w1, L0_ffn_b1, L0_ffn_w2, L0_ffn_b2)
    x = x + _L0_attn_ref(_layernorm(x, axis=-1), L0_attn_w_qkv, L0_attn_w_out)
    x = x + 0.5 * _L0_ffn_ref(_layernorm(x, axis=-1), L0_ffn_router_w, L0_ffn_w1, L0_ffn_b1, L0_ffn_w2, L0_ffn_b2)
    return x

_drawn_inputs = setup_inputs


def setup_inputs(seed=0):
    import zlib

    import numpy as np

    out = dict(_drawn_inputs(seed))
    spreads = {'L0_ffn_b1': (0.0, 0.711), 'L0_ffn_b2': (0.0, 0.684)}
    factors = {}
    for name, (base, spread) in spreads.items():
        noise = np.random.default_rng([zlib.crc32(name.encode()), seed]).standard_normal(out[name].shape)
        drawn = base * np.exp(spread * noise) if base else spread * noise
        out[name] = jnp.asarray(drawn.astype(out[name].dtype))
    for name, factor in factors.items():
        out[name] = (out[name] * factor).astype(out[name].dtype)
    return out
```

```python
import concourse.bass as bass
from concourse import mybir
from contextlib import ExitStack

FP32 = mybir.dt.float32
BF16 = mybir.dt.bfloat16
ALU = mybir.AluOpType
ACT = mybir.ActivationFunctionType
AX = mybir.AxisListType

P = 128
B, L, D = 4, 1024, 128
H, DH = 16, 8
LT = L // P
HALF = 512
NC = L // HALF
GH = 4
NG = H // GH
EPS = 1e-5
SCALE = float(DH) ** -0.5
STACK = 9 * DH
SHIFT = 96
KROWS = SHIFT + 3
SLOTS = 4
E, F = 14, 256
FC = F // P
TILES = B * LT
BLOCKS = TILES + E - 1
RING = 3
W1, B1 = 0, F
W2 = B1 + FC
B2 = W2 + FC * D
WX = B2 + D
assert BLOCKS % RING == 0
SHARED = 2 * GH * L + B * LT * D + 3 * L


class Memory:

    def __init__(self, nc, ctx):
        self.nc, self.ctx = nc, ctx

    def sb(self, name, shape, dt=FP32):
        return self.ctx.enter_context(self.nc.sbuf_tensor(name, shape, dt))

    def ps(self, name, shape, dt=FP32):
        return self.ctx.enter_context(self.nc.psum_tensor(name, shape, dt))

    def sem(self, name):
        return self.ctx.enter_context(self.nc.semaphore(name))


def over_batches(eng, batch):
    batch(0)
    with eng.Fori(1, B) as b:
        batch(b)


def wait_past(eng, sem, value):
    if not isinstance(value, int) or value > 0:
        eng.wait_ge(sem, value)


def setup_stage(nc, mem, x, w_qkv, w_out, cos, sin, consts):
    m = mem
    s_id = m.sem("identity_made")
    s_ld = m.sem("weights_loaded")
    s_x = m.sem("x_loaded")
    s_tr = m.sem("weights_transposed")
    s_ev = m.sem("weights_copied")
    s_neg = m.sem("weights_rotated")
    s_set = m.sem("constants_set")
    s_zero = m.sem("zeros_made")
    wraw = m.sb("w_raw", [P, 4, D])
    tp = m.st

    with nc.Block() as block:
        @block.sync
        def _(sp):
            sp.dma_start(wraw[:, 0:3, :], w_qkv.rearrange("(t p) d -> p t d", p=P)).then_inc(s_ld, 16)
            sp.dma_start(wraw[:, 3, :], w_out).then_inc(s_ld, 16)
            sp.dma_start(m.cos[:, :], cos).then_inc(s_x, 16)
            sp.dma_start(m.sin[:, :], sin).then_inc(s_x, 16)
            sp.dma_start(m.x[:, :, :, :], x.rearrange("b (i p) d -> p b i d", p=P)).then_inc(s_x, 16)
            sp.dma_start(m.consts[:, :], consts).then_inc(s_x, 16)
            sp.wait_ge(s_zero, 1)
            zeros = m.probs[:, 0:1, 0, 0:D].to_broadcast([P, BLOCKS, D])
            sp.dma_start(m.slots_in.rearrange("n p d -> p n d"), zeros).then_inc(s_x, 16)
            sp.wait_ge(s_x, 80)

        @block.gpsimd
        def _(pool):
            pool.memset(m.ident[:, :], 0.0).then_inc(s_id, 1)
            pool.wait_ge(s_id, 1)
            pool.affine_select(out=m.ident[:, :], in_=m.ident[:, :], compare_op=ALU.not_equal, fill=1.0,
                               base=0, pattern=[[-1, P]], channel_multiplier=1).then_inc(s_id, 1)
            pool.wait_ge(s_id, 2)
            pool.tensor_copy(m.ident_bf[:, :], m.ident[:, :]).then_inc(s_id, 1)
            for vg in range(2):
                pool.memset(m.vgroup[:, vg, :, :, :], 0.0).then_inc(s_set, 1)
            pool.wait_ge(s_set, 2)
            for vg in range(2):
                pool.memset(m.vgroup[:, vg, :, :, DH:DH + 1], 1.0).then_inc(s_set, 1)
            pool.memset(m.minus_half[:, :], -0.5).then_inc(s_set, 1)
            pool.memset(m.ones_bf[:, :], 1.0).then_inc(s_set, 1)
            pool.wait_ge(s_set, 6)
            pool.affine_select(out=m.upper[:, :], in_=m.ones_bf[:, :], compare_op=ALU.is_ge, fill=0.0,
                               base=0, pattern=[[1, P]], channel_multiplier=-1).then_inc(s_set, 1)
            pool.wait_ge(s_set, 7)
            pool.wait_ge(s_id, 3)

        @block.vector
        def _(dve):
            dve.memset(m.probs[:, 0, 0, 0:D], 0.0).then_inc(s_zero, 1)
            dve.memset(m.ones[:, :], 1.0)
            for s in range(4):
                dve.memset(m.qs[64:96, s, :, :], 0.0)
                dve.memset(m.ks[64:96, s, :, :], 0.0)
                last = dve.memset(m.ks[SHIFT:KROWS, s, :, :], 1.0)
            last.then_inc(s_neg, 1)
            dve.wait_ge(s_ev, 1)
            for half, src, sign in ((0, 1, -1.0), (1, 0, 1.0)):
                for n in range(2):
                    o = m.wrT[:, n, :].rearrange("p (h s d) -> p h s d", s=2, d=DH // 2)[:, :, half, :]
                    i = m.wT[:, n, :].rearrange("p (h s d) -> p h s d", s=2, d=DH // 2)[:, :, src, :]
                    last = dve.tensor_scalar(o, i, sign, None, ALU.mult)
            last.then_inc(s_neg, 1)
            dve.wait_ge(s_neg, 2)

        @block.tensor
        def _(pe):
            pe.wait_ge(s_ld, 32)
            pe.wait_ge(s_id, 2)
            for t in range(4):
                last = pe.transpose(tp[0][:, t * P:(t + 1) * P], wraw[:, t, :], m.ident[:, :])
            last.then_inc(s_tr, 1)

        @block.scalar
        def _(act):
            act.wait_ge(s_tr, 1)
            act.activation(m.wT[:, :, :], tp[0][:, :].rearrange("p (t d) -> p t d", t=4), ACT.Copy).then_inc(s_ev, 1)
            act.wait_ge(s_ev, 1)


def layer_norm_stats(dve, m, stats_done, step):
    for t in range(TILES):
        dve.bn_stats(m.stats[:, t, :], m.x[:, t // LT, t % LT, :]).then_inc(stats_done, 1)
    dve.wait_ge(stats_done, TILES)
    mean0, dev0, mean1, dev1 = (m.stats[:, :, n] for n in (1, 2, 4, 5))
    s, d, v, q = (m.ln_tmp[:, n, :] for n in range(4))
    dve.tensor_tensor(s, mean0, mean1, ALU.add).then_inc(step, 1)
    dve.tensor_tensor(d, mean0, mean1, ALU.subtract).then_inc(step, 1)
    dve.tensor_tensor(v, dev0, dev1, ALU.add).then_inc(step, 1)
    dve.wait_ge(step, 2)
    dve.tensor_tensor(q, d, d, ALU.mult).then_inc(step, 1)
    dve.tensor_scalar(m.mean[:, :], s, 0.5, None, ALU.mult).then_inc(step, 1)
    dve.wait_ge(step, 4)
    dve.scalar_tensor_tensor(out=d, in0=q, scalar=D / 4.0, in1=v, op0=ALU.mult, op1=ALU.add).then_inc(step, 1)
    dve.wait_ge(step, 6)
    dve.tensor_scalar(m.veps[:, :], d, 1.0 / D, EPS, ALU.mult, ALU.add).then_inc(step, 1)


def layer_norm_roots(pool, m, step, rstd_done):
    pool.wait_ge(step, 7)
    pool.tensor_tensor(m.rstd[:, :], m.veps[:, :], m.minus_half[:, :], ALU.pow).then_inc(rstd_done, 1)


def normalise(dve, m, b, xn, xn_done):
    for i in range(LT):
        t = b * LT + i
        dve.tensor_scalar(xn[:, i, :], m.x[:, b, i, :], m.mean[:, bass.ds(t, 1)], m.rstd[:, bass.ds(t, 1)],
                          ALU.subtract, ALU.mult).then_inc(xn_done, 1)


def ffn_stage(nc, mem, name, w1, b1, w2, b2, router):
    m = mem
    sem = lambda s: m.sem(f"{name}_{s}")
    stats_done, ln_step = sem("stats_done"), sem("ln_step")
    rstd_done, xn_done = sem("rstd_done"), sem("xn_done")
    router_loaded, bias_loaded, w_loaded = sem("router_loaded"), sem("bias_loaded"), sem("experts_loaded")
    bias_turned, bias_kept = sem("bias_turned"), sem("bias_kept")
    turned, kept, copied = sem("xn_turned"), sem("xnT_kept"), sem("xn_copied")
    logits_done = sem("logits_done")
    r = sem("routing_step")
    exped, prefixed, placed = sem("router_exp"), sem("prefixed"), sem("slots_placed")
    scattered = sem("rows_scattered")
    gathered = [sem(f"rows_gathered{b}") for b in range(B)]
    block_loaded = [sem(f"block{i}_loaded") for i in range(RING)]
    block_stored = [sem(f"block{i}_stored") for i in range(RING)]
    block_turned, block_kept = sem("block_turned"), sem("block_kept")
    w_copied = sem("block_weights_copied")
    hidden_done, gelu_done = sem("hidden_done"), sem("gelu_done")
    y_done, y_kept = sem("y_done"), sem("y_kept")
    combined = sem("combined")
    xs, ys = m.slots_in, m.slots_out

    logits = m.av[0][:, 0:TILES * E].rearrange("p (t e) -> p t e", e=E)
    prefix = m.mx[0][:, 0:TILES * E].rearrange("p (t e) -> p t e", e=E)
    totals = m.mx[0][:, HALF:HALF + TILES * E].rearrange("p (t e) -> p e t", e=E)
    own = [m.st[0][:, :], m.st[1][:, :], m.mx[0][:, 0:HALF]]
    yb = [m.av[0][:, 0:D], m.av[1][:, 0:D], m.mx[1][:, 0:D]]

    with nc.Block() as block:
        @block.sync
        def _(sp):
            sp.dma_start(m.router[:, :], router).then_inc(router_loaded, 16)
            sp.dma_start(m.b1_rows[:, :], b1.rearrange("e (c p) -> (e c) p", p=P)).then_inc(bias_loaded, 16)
            sp.dma_start(m.wx[:, :, W1:W1 + F], w1.rearrange("e p f -> p e f")).then_inc(w_loaded, 16)
            for c in range(FC):
                sp.dma_start(m.wx[:, :, W2 + c * D:W2 + (c + 1) * D],
                             w2[:, c * P:(c + 1) * P, :].rearrange("e p d -> p e d")).then_inc(w_loaded, 16)
            sp.dma_start(m.wx[:, :, B2:B2 + D], b2.unsqueeze(0).to_broadcast([P, E, D])).then_inc(w_loaded, 16)
            sp.wait_ge(scattered, 16 * TILES)

            def load(j, i):
                sp.dma_start(m.xblk[:, i, :], xs[j, :, :]).then_inc(block_loaded[i], 16)

            def store(j, i):
                sp.wait_ge(y_kept, j + 1)
                sp.dma_start(ys[j, :, :], m.yblk[:, i, :]).then_inc(block_stored[i], 16)

            for i in range(RING):
                load(i, i)
            with sp.Fori(0, BLOCKS // RING - 1) as it:
                for i in range(RING):
                    sp.wait_ge(block_turned, it * RING + i + 1)
                    load(it * RING + RING + i, i)
                    store(it * RING + i, i)
            for i in range(RING):
                store(BLOCKS - RING + i, i)
            for i in range(RING):
                sp.wait_ge(block_stored[i], 16 * (BLOCKS // RING))

        @block.gpsimd
        def _(pool):
            layer_norm_roots(pool, m, ln_step, rstd_done)
            def batch(b):
                pool.wait_ge(xn_done, b * LT + LT)
                pool.tensor_copy(m.rows[:, b, :, :], m.fxn[:, :, :]).then_inc(copied, 1)
            over_batches(pool, batch)
            pool.wait_ge(placed, 1)
            pool.wait_ge(copied, B)
            for t in range(TILES):
                pool.indirect_dma_start(xs.rearrange("n p d -> (n p) d"), bass.IndirectOffsetOnAxis(m.slot_i[:, t:t + 1], 0),
                                        m.rows[:, t // LT, t % LT, :], None).then_inc(scattered, 16)
            for i in range(RING):
                pool.wait_ge(block_stored[i], 16 * (BLOCKS // RING))
            for t in range(TILES):
                pool.indirect_dma_start(m.rows[:, t // LT, t % LT, :], None, ys.rearrange("n p d -> (n p) d"),
                                        bass.IndirectOffsetOnAxis(m.slot_i[:, t:t + 1], 0)).then_inc(gathered[t // LT], 16)

        @block.scalar
        def _(act):
            act.wait_ge(bias_turned, 1)
            act.activation(m.wx[:, :, B1:B1 + FC], m.av[1][:, 0:E * FC].rearrange("p (e c) -> p e c", c=FC),
                           ACT.Copy).then_inc(bias_kept, 1)
            def batch(b):
                for c in range(NC):
                    act.wait_ge(turned, NC * b + c + 1)
                    wait_past(act, logits_done, NC * b)
                    act.activation(m.xnT[:, c * HALF:(c + 1) * HALF], m.st[c][:, :], ACT.Copy).then_inc(kept, 1)
            over_batches(act, batch)
            act.wait_ge(r, 6)
            act.activation(m.rt[3][:, :, :], m.rt[2][:, :, :], ACT.Exp).then_inc(exped, 1)

            def gelu(j, i):
                act.wait_ge(hidden_done, j + 1)
                for c in range(FC):
                    last = act.activation(m.hid[:, i, c, :], own[i][:, P * (c + 1):P * (c + 2)], ACT.Gelu,
                                          bias=m.wblk[:, i, B1 + c:B1 + c + 1])
                last.then_inc(gelu_done, 1)
            for i in range(RING):
                gelu(i, i)
            with act.Fori(1, BLOCKS // RING) as it:
                for i in range(RING):
                    gelu(it * RING + i, i)

        @block.tensor
        def _(pe):
            pe.wait_ge(bias_loaded, 16)
            pe.transpose(m.av[1][:, 0:E * FC], m.b1_rows[:, :], m.ident[0:E * FC, 0:E * FC]).then_inc(bias_turned, 1)
            pe.wait_ge(router_loaded, 16)
            def batch(b):
                for c in range(NC):
                    pe.wait_ge(xn_done, LT * b + 4 * c + 4)
                    wait_past(pe, kept, NC * b)
                    for t in range(4):
                        last = pe.transpose(m.st[c][:, t * P:(t + 1) * P], m.fxn[:, 4 * c + t, :], m.ident[:, :])
                    last.then_inc(turned, 1)
                for c in range(NC):
                    pe.wait_ge(kept, NC * b + c + 1)
                    for t in range(4):
                        i = 4 * c + t
                        last = pe.matmul(logits[:, b * LT + i, :], m.xnT[:, i * P:(i + 1) * P], m.router[:, :],
                                         start=True, stop=True)
                    last.then_inc(logits_done, 1)
            over_batches(pe, batch)
            pe.wait_ge(r, 5)
            choice = m.choice[:, :, :].rearrange("p t e -> p (t e)")
            pe.matmul(m.mx[0][:, 0:TILES * E], m.upper[:, :], choice, start=True, stop=True)
            pe.matmul(m.mx[0][:, HALF:HALF + TILES * E], m.ones_bf[:, :], choice, start=True, stop=True).then_inc(prefixed, 1)

            def step(k, i, turn, up, down):
                if turn:
                    pe.wait_ge(block_loaded[i], 16 * m.round[0] + 16)
                    if not isinstance(k, int) or k >= RING:
                        pe.wait_ge(gelu_done, k - RING + 1)
                    pe.transpose(own[i][:, 0:P], m.xblk[:, i, :], m.ident[:, :]).then_inc(block_turned, 1)
                if up:
                    q = (i - 1) % RING
                    pe.wait_ge(block_kept, k)
                    pe.wait_ge(w_copied, k)
                    for c in range(FC):
                        last = pe.matmul(own[q][:, P * (c + 1):P * (c + 2)], m.wblk[:, q, W1 + c * P:W1 + (c + 1) * P],
                                         m.xT[:, q, :], start=True, stop=True)
                    last.then_inc(hidden_done, 1)
                if down:
                    q = (i - 2) % RING
                    pe.wait_ge(gelu_done, k - 1)
                    if not isinstance(k, int) or k > RING:
                        pe.wait_ge(y_kept, k - RING)
                    for c in range(FC):
                        last = pe.matmul(yb[q], m.hid[:, q, c, :], m.wblk[:, q, W2 + c * D:W2 + (c + 1) * D],
                                         start=(c == 0), stop=(c == FC - 1))
                    last.then_inc(y_done, 1)
            for k in range(2 * RING):
                m.round = [k // RING]
                step(k, k % RING, True, k >= 1, k >= 2)
            with pe.Fori(2, BLOCKS // RING) as it:
                m.round = [it]
                for i in range(RING):
                    step(it * RING + i, i, True, True, True)
            step(BLOCKS, 0, False, True, True)
            step(BLOCKS + 1, 1, False, False, True)

        @block.vector
        def _(dve):
            layer_norm_stats(dve, m, stats_done, ln_step)
            dve.wait_ge(rstd_done, 1)
            def batch(b):
                wait_past(dve, copied, b)
                wait_past(dve, turned, NC * b)
                normalise(dve, m, b, m.fxn, xn_done)
            over_batches(dve, batch)
            dve.wait_ge(logits_done, NC * B)
            T = m.rt
            count = [0]

            def step(make, *args, **kw):
                if count[0]:
                    dve.wait_ge(r, count[0])
                make(*args, **kw).then_inc(r, 1)
                count[0] += 1

            def over_e(a):
                return a.unsqueeze(2).to_broadcast([P, TILES, E])

            def over_t(a):
                return a.unsqueeze(1).to_broadcast([P, TILES, E])
            flip = lambda a: a.rearrange("p t e -> p (t e)").rearrange("p (e t) -> p e t", e=E)
            step(dve.tensor_reduce, m.tmax[:, :], logits, AX.X, ALU.max)
            step(dve.tensor_tensor, T[0][:, :, :], logits, over_e(m.tmax[:, :]), ALU.is_equal)
            step(dve.tensor_tensor, T[1][:, :, :], T[0][:, :, :], over_t(m.consts[:, 0:E]), ALU.mult)
            step(dve.tensor_reduce, m.tfirst[:, :], T[1][:, :, :], AX.X, ALU.max)
            step(dve.tensor_tensor, m.choice[:, :, :], over_t(m.consts[:, 0:E]), over_e(m.tfirst[:, :]), ALU.is_equal)
            step(dve.tensor_tensor, T[2][:, :, :], logits, over_e(m.tmax[:, :]), ALU.subtract)
            dve.wait_ge(prefixed, 1)
            tot, cum, base = flip(T[0][:, :, :]), flip(T[1][:, :, :]), flip(T[4][:, :, :])
            step(dve.tensor_copy, tot, totals)
            step(dve.tensor_tensor_scan, cum.rearrange("p e t -> p (e t)"), m.ones[:, 0:TILES * E],
                 tot.rearrange("p e t -> p (e t)"), 0.0, ALU.mult, ALU.add)
            cnt, nb, bend, t1, t2 = (m.per_e[:, n, :] for n in range(5))
            step(dve.tensor_reduce, cnt, tot, AX.X, ALU.add)
            step(dve.tensor_tensor, base, cnt.unsqueeze(2).to_broadcast([P, E, TILES]),
                 m.consts[:, E:E + TILES].unsqueeze(1).to_broadcast([P, E, TILES]), ALU.is_gt)
            step(dve.tensor_reduce, nb, base, AX.X, ALU.add)
            step(dve.tensor_tensor_scan, bend, m.ones[:, 0:E], nb, 0.0, ALU.mult, ALU.add)
            step(dve.tensor_tensor, t1, bend, nb, ALU.subtract)
            step(dve.scalar_tensor_tensor, out=t2, in0=cum[:, :, TILES - 1], scalar=1.0, in1=cnt, op0=ALU.add, op1=ALU.subtract)
            step(dve.scalar_tensor_tensor, out=t1, in0=t1, scalar=float(P), in1=t2, op0=ALU.mult, op1=ALU.subtract)
            step(dve.tensor_tensor, cum, cum, tot, ALU.subtract)
            step(dve.tensor_tensor, base, cum, t1.unsqueeze(2).to_broadcast([P, E, TILES]), ALU.add)
            step(dve.tensor_tensor, T[0][:, :, :], prefix, base.rearrange("p e t -> p t e"), ALU.add)
            step(dve.tensor_tensor, T[1][:, :, :], T[0][:, :, :], m.choice[:, :, :], ALU.mult)
            step(dve.tensor_reduce, m.slot_f[:, :], T[1][:, :, :], AX.X, ALU.add)
            dve.wait_ge(r, count[0])
            dve.tensor_copy(m.slot_i[:, :], m.slot_f[:, :]).then_inc(placed, 1)
            last_block = m.block_cmp[:, :, :]
            step(dve.tensor_tensor, last_block, bend[0:1, :].unsqueeze(1).to_broadcast([1, BLOCKS, E]),
                 m.consts[0:1, E + TILES:E + TILES + BLOCKS].unsqueeze(2).to_broadcast([1, BLOCKS, E]), ALU.is_le)
            step(dve.tensor_reduce, m.block_f[:, :], last_block, AX.X, ALU.add)
            step(dve.tensor_scalar, m.block_e[:, :], m.block_f[:, :], float(E - 1), None, ALU.min)
            dve.wait_ge(exped, 1)
            step(dve.tensor_reduce, m.psum_e[:, :], T[3][:, :, :], AX.X, ALU.add)
            step(dve.reciprocal, m.tmax[:, :], m.psum_e[:, :])
            step(dve.tensor_scalar, m.half_p[:, :], m.tmax[:, :], 0.5, None, ALU.mult)
            dve.wait_ge(r, count[0])
            dve.wait_ge(w_loaded, 16 * (2 + FC))
            dve.wait_ge(bias_kept, 1)

            def turn(k, i):
                dve.wait_ge(block_turned, k + 1)
                dve.tensor_copy(m.xT[:, i, :], own[i][:, 0:P]).then_inc(block_kept, 1)
                if not isinstance(k, int) or k >= RING:
                    dve.wait_ge(y_kept, k - RING + 1)
                e = dve.value_load(m.block_e[0:1, bass.ds(k, 1)], min_val=0, max_val=E - 1)
                dve.tensor_copy(m.wblk[:, i, :], m.wx[:, e, :]).then_inc(w_copied, 1)

            def keep(j, i, full):
                dve.wait_ge(y_done, j + 1)
                if full is not None:
                    dve.wait_ge(block_stored[i], full)
                dve.tensor_tensor(m.yblk[:, i, :], yb[i], m.wblk[:, i, B2:B2 + D], ALU.add).then_inc(y_kept, 1)
            for k in range(2 * RING):
                turn(k, k % RING)
                if k >= 2:
                    keep(k - 2, (k - 2) % RING, 16 if k - 2 >= RING else None)
            with dve.Fori(2, BLOCKS // RING) as it:
                for i in range(RING):
                    turn(it * RING + i, i)
                    q = (i - 2) % RING
                    keep(it * RING + i - 2, q, (it - 1) * 16 if q > i else it * 16)
            keep(BLOCKS - 2, 1, 16 * (BLOCKS // RING - 1))
            keep(BLOCKS - 1, 2, 16 * (BLOCKS // RING - 1))
            for b in range(B):
                dve.wait_ge(gathered[b], 16 * LT)
                for i in range(LT):
                    t = LT * b + i
                    dve.scalar_tensor_tensor(out=m.x[:, b, i, :], in0=m.rows[:, b, i, :], scalar=m.half_p[:, t:t + 1],
                                             in1=m.x[:, b, i, :], op0=ALU.mult, op1=ALU.add).then_inc(combined, 1)
            dve.wait_ge(combined, TILES)


def project_stage(nc, mem):
    m = mem
    stats_done = m.sem("stats_done")
    ln_step = m.sem("ln_step")
    rstd_done = m.sem("rstd_done")
    xn_done = m.sem("xn_done")
    xn_turned = m.sem("xn_turned")
    xnT_done = m.sem("xnT_done")
    proj_done = m.sem("proj_done")
    v_done = m.sem("v_projected")
    v_kept = m.sem("v_kept")
    scaled = m.sem("rope_products")
    roped = m.sem("roped")
    hi_done = m.sem("hi_done")
    rest1 = m.sem("rest1_done")
    mid_done = m.sem("mid_done")
    lo_done = m.sem("lo_done")
    stored = m.sem("parts_stored")
    STORES = 12 * 16

    banks = [[m.mx[0][:, 0:HALF], m.mx[0][:, HALF:], m.mx[1][:, 0:HALF], m.mx[1][:, HALF:]],
             [m.av[0][:, :], m.av[1][:, :], m.st[0][:, :], m.st[1][:, :]]]

    with nc.Block() as block:
        @block.vector
        def _(dve):
            layer_norm_stats(dve, m, stats_done, ln_step)
            dve.wait_ge(rstd_done, 1)
            def batch(b):
                wait_past(dve, xn_turned, NC * b)
                normalise(dve, m, b, m.xn, xn_done)
                for c in range(NC):
                    dve.wait_ge(proj_done, b * NC + c + 1)
                    wait_past(dve, roped, (b * NC + c) * 2)
                    cs = slice(c * HALF, (c + 1) * HALF)
                    for n in range(2):
                        dve.tensor_tensor(m.tcos[:, n, :], banks[c][2 * n], m.cos[:, cs], ALU.mult).then_inc(scaled, 1)
                        dve.tensor_tensor(m.tsin[:, n, :], banks[c][2 * n + 1], m.sin[:, cs], ALU.mult).then_inc(scaled, 1)
                    for n in range(2):
                        dve.wait_ge(scaled, (b * NC + c) * 4 + 2 * n + 2)
                        wait_past(dve, lo_done, (b * NC + c) * 2)
                        dve.tensor_tensor(m.roped[:, n, :], m.tcos[:, n, :], m.tsin[:, n, :], ALU.add).then_inc(roped, 1)
                for c in range(NC):
                    dve.wait_ge(v_done, b * NC + c + 1)
                    dve.tensor_copy(m.v[:, b, 4 * c:4 * c + 4, :], banks[0][c].rearrange("p (t d) -> p t d", d=D)).then_inc(v_kept, 1)
            over_batches(dve, batch)

        @block.tensor
        def _(pe):
            def batch(b):
                for c in range(NC):
                    pe.wait_ge(xn_done, b * LT + 4 * c + 4)
                    wait_past(pe, scaled, b * 8)
                    for t in range(4):
                        last = pe.transpose(m.st[c][:, t * P:(t + 1) * P], m.xn[:, 4 * c + t, :], m.ident[:, :])
                    last.then_inc(xn_turned, 1)
                for c in range(NC):
                    pe.wait_ge(xnT_done, b * NC + NC)
                    wait_past(pe, v_kept, b * NC)
                    cs = slice(c * HALF, (c + 1) * HALF)
                    for n in range(2):
                        pe.matmul(banks[c][2 * n], m.wT[:, n, :], m.xnT[:, cs], start=True, stop=True)
                        last = pe.matmul(banks[c][2 * n + 1], m.wrT[:, n, :], m.xnT[:, cs], start=True, stop=True)
                    last.then_inc(proj_done, 1)
                pe.wait_ge(scaled, b * 8 + 4)
                for c in range(NC):
                    for t in range(4):
                        i = 4 * c + t
                        last = pe.matmul(banks[0][c][:, t * P:(t + 1) * P], m.xnT[:, i * P:(i + 1) * P], m.wT[:, 2, :],
                                         start=True, stop=True)
                    last.then_inc(v_done, 1)
            over_batches(pe, batch)

        @block.scalar
        def _(act):
            def batch(b):
                for c in range(NC):
                    act.wait_ge(xn_turned, b * NC + c + 1)
                    wait_past(act, v_done, b * NC)
                    act.activation(m.xnT[:, c * HALF:(c + 1) * HALF], m.st[c][:, :], ACT.Copy).then_inc(xnT_done, 1)
                wait_past(act, stored, b * STORES)
                for c in range(NC):
                    cs = slice(c * HALF, (c + 1) * HALF)
                    for n in range(2):
                        k = 2 * c + n + 1
                        act.wait_ge(roped, b * 4 + k)
                        act.activation(m.parts[:, n, 0, cs], m.roped[:, n, :], ACT.Copy).then_inc(hi_done, 1)
                    for n in range(2):
                        k = 2 * c + n + 1
                        act.wait_ge(rest1, b * 4 + k)
                        act.activation(m.parts[:, n, 1, cs], m.rest[:, n, :], ACT.Copy).then_inc(mid_done, 1)
            over_batches(act, batch)

        @block.gpsimd
        def _(pool):
            layer_norm_roots(pool, m, ln_step, rstd_done)
            def batch(b):
                for c in range(NC):
                    cs = slice(c * HALF, (c + 1) * HALF)
                    for n in range(2):
                        k = 2 * c + n + 1
                        pool.wait_ge(hi_done, b * 4 + k)
                        wait_past(pool, lo_done, b * 4 + 2 * c)
                        pool.tensor_tensor(m.rest[:, n, :], m.roped[:, n, :], m.parts[:, n, 0, cs], ALU.subtract).then_inc(rest1, 1)
                    for n in range(2):
                        k = 2 * c + n + 1
                        pool.wait_ge(mid_done, b * 4 + k)
                        pool.tensor_tensor(m.parts[:, n, 2, cs], m.rest[:, n, :], m.parts[:, n, 1, cs], ALU.subtract).then_inc(lo_done, 1)
            over_batches(pool, batch)

        @block.sync
        def _(sp):
            def batch(b):
                sp.wait_ge(lo_done, b * 4 + 4)
                sp.wait_ge(mid_done, b * 4 + 4)
                sp.wait_ge(hi_done, b * 4 + 4)
                for part in range(3):
                    for copy in range(3):
                        sp.dma_start(m.q_store(b, part, copy), m.parts[:, 0, part, :]).then_inc(stored, 16)
                    sp.dma_start(m.k_store(b, part), m.parts[:, 1, part, :]).then_inc(stored, 16)
            over_batches(sp, batch)
            sp.wait_ge(stored, B * STORES)


def attention_stage(nc, mem):
    m = mem
    stack_loaded = [m.sem(f"stack{s}_loaded") for s in range(SLOTS)]
    shift_loaded = [m.sem(f"shift{s}_loaded") for s in range(SLOTS)]
    v_ready = m.sem("v_group_ready")
    turn_full = m.sem("turn_full")
    turn_free = m.sem("turn_free")
    score_full = m.sem("score_full")
    exp_done = m.sem("exp_done")
    pv_done = m.sem("pv_done")
    av_kept = m.sem("av_kept")
    split = m.sem("shift_split")
    shift_made = m.sem("shift_made")
    shift_kept = m.sem("shift_kept")
    recip_done = m.sem("recip_done")
    ITEMS = GH * LT
    EARLY = 8
    BODY = ITEMS + 2
    FIRST = ITEMS + 1 + EARLY
    CH = GH * NC

    def schedule(G, has_next, has_second):
        out = {p: [] for p in range(1, LT + 1)}
        if has_next:
            for p in range(1, LT - 1):
                out[p] += [("max", 1, EARLY + 4 * (p - 1) + j) for j in range(4)]
            out[LT - 1].append(("shift", 1, 0))
        if has_second:
            out[LT - 1] = [("max", 2, 0), ("max", 2, 1)] + out[LT - 1] + [("max", 2, 2), ("max", 2, 3)]
            out[LT] += [("max", 2, 4 + j) for j in range(4)]
        out[LT].append(("avt", 0, 0))
        return out

    def first_turn(b, u):
        short = EARLY if isinstance(b, int) and b == B - 1 and u == NG - 1 else 0
        return FIRST + BODY * (NG * b + u) - short

    def place(b, u, ahead):
        return (b + 1, u + ahead - NG) if u + ahead >= NG else (b, u + ahead)

    def turn_pe(pe, b, u, n, turn, slot):
        kind, ahead, j = turn
        bb, uu = place(b, u, ahead)
        if not isinstance(n, int) or n >= 2:
            pe.wait_ge(turn_free, n - 1)
        out = m.mx[slot]
        if kind == "max":
            h, qt = j // LT, j % LT
            if j == 0:
                pe.wait_ge(stack_loaded[uu], 64 * (bb + 1))
            for c in range(NC):
                last = pe.matmul(out[:, c * HALF:(c + 1) * HALF], m.qs[0:SHIFT, uu, h, qt * P:(qt + 1) * P],
                                 m.ks[0:SHIFT, uu, h, c * HALF:(c + 1) * HALF], start=True, stop=True)
                if c == 0:
                    yield
        elif kind == "shift":
            pe.wait_ge(shift_made, 4 * bb + uu + 1)
            last = pe.transpose(out[0:3 * ITEMS, 0:P // 2].bitcast(BF16), m.m3[:, :], m.ident_bf[:, :])
        else:
            pe.wait_ge(av_kept, 2 * (4 * bb + uu) + 3)
            for qt in range(LT):
                last = pe.transpose(out[:, qt * P:(qt + 1) * P],
                                    m.avs[:, qt // 4, (qt % 4) * P:(qt % 4 + 1) * P], m.ident[:, :])
        last.then_inc(turn_full, 1)

    def turn_dve(dve, b, u, n, turn, slot):
        kind, ahead, j = turn
        bb, uu = place(b, u, ahead)
        g = 4 * bb + uu
        dve.wait_ge(turn_full, n + 1)
        src = m.mx[slot]
        if kind == "max":
            if j == 0:
                dve.wait_ge(shift_made, g)
            dve.tensor_reduce(m.maxima[:, j:j + 1], src[:, :], AX.X, ALU.max).then_inc(turn_free, 1)
            if j == ITEMS - 1:
                dve.wait_ge(turn_free, n + 1)
                dve.tensor_scalar(m.m3[:, 0:ITEMS], m.maxima[:, :], -1.0, None, ALU.mult).then_inc(split, 1)
                dve.wait_ge(split, 3 * g + 1)
                dve.scalar_tensor_tensor(out=m.mrest[:, :], in0=m.maxima[:, :], scalar=-1.0, in1=m.m3[:, 0:ITEMS],
                                         op0=ALU.mult, op1=ALU.subtract).then_inc(split, 1)
                dve.wait_ge(split, 3 * g + 2)
                dve.tensor_copy(m.m3[:, ITEMS:2 * ITEMS], m.mrest[:, :]).then_inc(split, 1)
                dve.wait_ge(split, 3 * g + 3)
                dve.tensor_tensor(m.m3[:, 2 * ITEMS:3 * ITEMS], m.mrest[:, :], m.m3[:, ITEMS:2 * ITEMS],
                                  ALU.subtract).then_inc(shift_made, 1)
        elif kind == "shift":
            if not (isinstance(g, int) and g == 0):
                pb, pu = (bb, uu - 1) if uu else (bb - 1, NG - 1)
                dve.wait_ge(shift_loaded[pu], 48 * (pb + 1))
            dve.tensor_copy(m.m3T[:, :], src[0:3 * ITEMS, 0:P // 2].bitcast(BF16)).then_inc(turn_free, 1)
        else:
            t = src[:, :].rearrange("p (q h r) -> p q h r", h=GH, r=32)
            dve.wait_ge(turn_free, n)
            dve.reciprocal(m.recip[:, :, :], t[:, :, :, DH]).then_inc(recip_done, 1)
            dve.wait_ge(recip_done, g + 1)
            o = m.attn[:, bb, :, uu * GH * DH:(uu + 1) * GH * DH].rearrange("p q (h d) -> p q h d", d=DH)
            dve.tensor_tensor(o, t[:, :, :, 0:DH], m.recip[:, :, :].unsqueeze(3).to_broadcast([P, LT, GH, DH]),
                              ALU.mult).then_inc(turn_free, 1)

    def scores(pe, b, u, s, c, h):
        k = CH * (LT * (4 * b + u) + s) + GH * c + h
        if not isinstance(k, int) or k >= 2:
            pe.wait_ge(exp_done, k - 1)
        if s == 0 and c == 0 and h == 0:
            pe.wait_ge(shift_loaded[u], 48 * (b + 1))
        pe.matmul(m.st[h % 2][:, :], m.ks[0:KROWS, u, h, s * P:(s + 1) * P], m.qs[0:KROWS, u, h, c * HALF:(c + 1) * HALF],
                  start=True, stop=True).then_inc(score_full, 1)

    def product(pe, b, u, s, c):
        g = 4 * b + u
        if s == 0 and c == 0:
            pe.wait_ge(v_ready, g + 1)
            pe.wait_ge(av_kept, 2 * g + 1)
        pe.wait_ge(exp_done, CH * (LT * g + s) + GH * (c + 1))
        for h in range(GH):
            last = pe.matmul(m.av[c][32 * h:32 * h + 32, :], m.vgroup[:, u % 2, s, h, :],
                             m.probs[:, s % 2, h, c * HALF:(c + 1) * HALF], start=(s == 0), stop=(s == LT - 1))
        last.then_inc(pv_done, 1)

    def body_pe(pe, b, u, has_next, has_second):
        n = first_turn(b, u)
        k = 0
        for pos, lst in schedule(u, has_next, has_second).items():
            turns = []
            for turn in lst:
                turns.append(turn_pe(pe, b, u, n + k, turn, (FIRST + k) % 2))
                k += 1
            at = 0
            for c in range(NC):
                product(pe, b, u, pos - 1, c)
                for h in range(GH):
                    if pos < LT:
                        scores(pe, b, u, pos, c, h)
                    elif has_next:
                        scores(pe, *place(b, u, 1), 0, c, h)
                    if turns and not (lst[at][0] == "avt"):
                        if next(turns[0], "end") == "end":
                            turns.pop(0)
                            at += 1
            for t in turns:
                for _ in t:
                    pass

    def body_act(act, b, u, has_next):
        for pos in range(1, LT + 1):
            for c in range(NC):
                if pos < LT:
                    exps(act, b, u, pos, c)
                elif has_next:
                    exps(act, *place(b, u, 1), 0, c)
                if pos == LT:
                    act.wait_ge(pv_done, 2 * (LT * (4 * b + u) + LT - 1) + c + 2)
                    act.activation(m.avs[:, c, :], m.av[c][:, :], ACT.Copy).then_inc(av_kept, 1)

    def exps(act, b, u, s, c):
        for h in range(GH):
            act.wait_ge(score_full, CH * (LT * (4 * b + u) + s) + GH * c + h + 1)
            act.activation(m.probs[:, s % 2, h, c * HALF:(c + 1) * HALF], m.st[h % 2][:, :], ACT.Exp,
                           scale=SCALE).then_inc(exp_done, 1)

    def first_turns():
        return [("max", 0, j) for j in range(ITEMS)] + [("max", 1, j) for j in range(2)] + [("shift", 0, 0)] + \
               [("max", 1, j) for j in range(2, EARLY)]

    def bodies(f):
        def run(eng):
            with eng.Fori(0, B - 1) as b:
                for u in range(NG):
                    f(eng, b, u, True, True)
            for u in range(NG):
                f(eng, B - 1, u, u < NG - 1, u < NG - 2)
        return run

    def load_stack(sp, b, u):
        sp.dma_start(m.qs[0:STACK, u, :, :], m.stack_q(b, u)).then_inc(stack_loaded[u], 16)
        for copy in range(3):
            rows = slice(3 * DH * copy, 3 * DH * (copy + 1))
            sp.dma_start(m.ks[rows, u, :, :], m.stack_k(b, u)).then_inc(stack_loaded[u], 16)

    def load_shift(sp, b, u):
        sp.wait_ge(turn_free, shift_turn(b, u) + 1)
        for part in range(3):
            sp.dma_start(m.qs[SHIFT + part:SHIFT + part + 1, u, :, :].rearrange("o h (q t) -> o (h q) t", t=P),
                         m.m3T[part * ITEMS:(part + 1) * ITEMS, :]).then_inc(shift_loaded[u], 16)

    def shift_turn(b, u):
        if isinstance(b, int) and b == 0 and u == 0:
            return ITEMS + 2
        pb, pu = (b, u - 1) if u else (b - 1, NG - 1)
        last = isinstance(pb, int) and pb == B - 1 and pu == NG - 2
        before = 4 * (LT - 2) + (0 if last else 2)
        return first_turn(pb, pu) + before

    with nc.Block() as block:
        @block.tensor
        def _(pe):
            pe.sem_inc(pv_done, 1)
            for n, turn in enumerate(first_turns()):
                for _ in turn_pe(pe, 0, 0, n, turn, n % 2):
                    pass
            for c in range(NC):
                for h in range(GH):
                    scores(pe, 0, 0, 0, c, h)
            bodies(body_pe)(pe)

        @block.vector
        def _(dve):
            for n, turn in enumerate(first_turns()):
                turn_dve(dve, 0, 0, n, turn, n % 2)

            def body(eng, b, u, has_next, has_second):
                n = first_turn(b, u)
                lst = [t for x in schedule(u, has_next, has_second).values() for t in x]
                for k, turn in enumerate(lst):
                    turn_dve(eng, b, u, n + k, turn, (FIRST + k) % 2)
            bodies(body)(dve)

        @block.scalar
        def _(act):
            act.sem_inc(av_kept, 1)
            for c in range(NC):
                exps(act, 0, 0, 0, c)
            bodies(lambda eng, b, u, has_next, _: body_act(eng, b, u, has_next))(act)

        @block.gpsimd
        def _(pool):
            def copy_v(b, u):
                pool.tensor_copy(m.vgroup[:, u % 2, :, :, 0:DH],
                                 m.v[:, b, :, u * GH * DH:(u + 1) * GH * DH].rearrange("p t (h d) -> p t h d", d=DH))\
                    .then_inc(v_ready, 1)
            copy_v(0, 0)

            def body(eng, b, u, has_next, _):
                if has_next:
                    eng.wait_ge(pv_done, 2 * LT * (4 * b + u) + 1)
                    copy_v(*place(b, u, 1))
            bodies(body)(pool)

        @block.sync
        def _(sp):
            load_stack(sp, 0, 0)
            load_stack(sp, 0, 1)
            load_shift(sp, 0, 0)

            def body(eng, b, u, has_next, has_second):
                if has_second:
                    load_stack(eng, *place(b, u, 2))
                if has_next:
                    load_shift(eng, *place(b, u, 1))
            bodies(body)(sp)
            for s in range(SLOTS):
                sp.wait_ge(shift_loaded[s], 48 * B)


def output_stage(nc, mem):
    m = mem
    turned = m.sem("attn_turned")
    kept = m.sem("attnT_kept")
    out_done = m.sem("out_projected")
    added = m.sem("x_added")
    with nc.Block() as block:
        @block.tensor
        def _(pe):
            for b in range(B):
                for c in range(NC):
                    wait_past(pe, kept, NC * b)
                    for t in range(4):
                        last = pe.transpose(m.st[c][:, t * P:(t + 1) * P], m.attn[:, b, 4 * c + t, :], m.ident[:, :])
                    last.then_inc(turned, 1)
                for c in range(NC):
                    pe.wait_ge(kept, NC * b + c + 1)
                    wait_past(pe, added, NC * b)
                    for t in range(4):
                        last = pe.matmul(m.av[c][:, t * P:(t + 1) * P], m.xnT[:, (4 * c + t) * P:(4 * c + t + 1) * P],
                                         m.wT[:, 3, :], start=True, stop=True)
                    last.then_inc(out_done, 1)

        @block.scalar
        def _(act):
            for b in range(B):
                for c in range(NC):
                    act.wait_ge(turned, NC * b + c + 1)
                    wait_past(act, out_done, NC * b)
                    act.activation(m.xnT[:, c * HALF:(c + 1) * HALF], m.st[c][:, :], ACT.Copy).then_inc(kept, 1)

        @block.vector
        def _(dve):
            for b in range(B):
                for c in range(NC):
                    dve.wait_ge(out_done, NC * b + c + 1)
                    xs = m.x[:, b, 4 * c:4 * c + 4, :]
                    dve.tensor_tensor(xs, m.av[c][:, :].rearrange("p (t d) -> p t d", d=D), xs, ALU.add).then_inc(added, 1)
            dve.wait_ge(added, NC * B)


def program(nc, x, w_qkv, w_out, router, w1, b1, w2, b2, cos, sin, consts, out):
    with ExitStack() as ctx:
        m = Memory(nc, ctx)
        q_parts = nc.dram_tensor("q_parts", (B, H, STACK, L), BF16, kind="Internal").ap()
        k_parts = nc.dram_tensor("k_parts", (B, H, 3 * DH, L), BF16, kind="Internal").ap()

        def q_store(b, part, copy):
            r = (3 * part + copy) * DH
            return q_parts[b, :, r:r + DH, :]

        def k_store(b, part):
            return k_parts[b, :, part * DH:(part + 1) * DH, :]

        def stack_q(b, u):
            return q_parts[b, u * GH:(u + 1) * GH, :, :].rearrange("h r t -> r h t")

        def stack_k(b, u):
            return k_parts[b, u * GH:(u + 1) * GH, :, :].rearrange("h r t -> r h t")

        m.q_store, m.k_store, m.stack_q, m.stack_k = q_store, k_store, stack_q, stack_k
        m.x = m.sb("x_tokens", [P, B, LT, D])
        m.ident = m.sb("identity", [P, P])
        m.ident_bf = m.sb("identity_bf", [P, P], BF16)
        m.wT = m.sb("w_transposed", [P, 4, D])
        m.wrT = m.sb("w_rotated", [P, 2, D])
        m.cos = m.sb("rope_cos", [P, L])
        m.sin = m.sb("rope_sin", [P, L])
        m.stats = m.sb("ln_stats", [P, TILES, 6])
        m.ln_tmp = m.sb("ln_steps", [P, 4, TILES])
        m.mean = m.sb("ln_mean", [P, TILES])
        m.veps = m.sb("ln_var_eps", [P, TILES])
        m.rstd = m.sb("ln_rstd", [P, TILES])
        m.minus_half = m.sb("minus_half", [P, TILES])
        m.xnT = m.sb("xn_transposed", [P, L])
        m.attn = m.sb("attn_tokens", [P, B, LT, D])
        m.qs = m.sb("q_stacks", [KROWS, SLOTS, GH, L], BF16)
        m.ks = m.sb("k_stacks", [KROWS, SLOTS, GH, L], BF16)
        m.vgroup = m.sb("v_group", [P, 2, LT, GH, 32])
        m.maxima = m.sb("maxima", [P, GH * LT])
        m.mrest = m.sb("maxima_rest", [P, GH * LT])
        m.m3 = m.sb("maxima_parts", [P, 3 * GH * LT], BF16)
        m.m3T = m.sb("maxima_rows", [3 * GH * LT, P], BF16)
        m.avs = m.sb("av_sums", [P, NC, HALF])
        m.recip = m.sb("sum_recips", [P, LT, GH])
        m.st = [m.ps(f"scores{i}", [P, HALF]) for i in range(2)]
        m.mx = [m.ps(f"turn{i}", [P, L]) for i in range(2)]
        m.av = [m.ps(f"av{i}", [P, HALF]) for i in range(2)]
        shared = m.sb("shared", [P, SHARED])
        at = [0]

        def take(n):
            at[0] += n
            assert at[0] <= SHARED
            return shared[:, at[0] - n:at[0]]
        m.probs = take(2 * GH * L).rearrange("p (s h t) -> p s h t", s=2, h=GH)
        m.v = take(B * LT * D).rearrange("p (b i d) -> p b i d", b=B, i=LT)
        m.parts = take(3 * L).bitcast(BF16).rearrange("p (n i t) -> p n i t", n=2, i=3)
        m.xn = m.probs[:, 0, 0, :].rearrange("p (i d) -> p i d", d=D)
        m.tcos = m.probs[:, 0, 1, :].rearrange("p (n t) -> p n t", n=2)
        m.tsin = m.probs[:, 0, 2, :].rearrange("p (n t) -> p n t", n=2)
        m.roped = m.probs[:, 0, 3, :].rearrange("p (n t) -> p n t", n=2)
        m.rest = m.probs[:, 1, 0, :].rearrange("p (n t) -> p n t", n=2)
        at[0] = 0
        m.wx = take(E * WX).rearrange("p (e w) -> p e w", e=E)
        m.fxn = take(LT * D).rearrange("p (i d) -> p i d", d=D)
        m.hid = take(RING * F).rearrange("p (r c t) -> p r c t", r=RING, c=FC)
        m.wblk = take(RING * WX).rearrange("p (r w) -> p r w", r=RING)
        m.xblk = take(RING * D).rearrange("p (r d) -> p r d", r=RING)
        m.yblk = take(RING * D).rearrange("p (r d) -> p r d", r=RING)
        m.xT = take(RING * P).rearrange("p (r d) -> p r d", r=RING)
        m.rows = m.attn
        m.router = m.sb("router", [P, E])
        m.b1_rows = m.sb("b1_rows", [E * FC, P])
        m.rt = [m.sb(f"routing{i}", [P, TILES, E]) for i in range(5)]
        m.choice = m.sb("choice", [P, TILES, E], BF16)
        m.ones = m.sb("ones", [P, TILES * E])
        m.ones_bf = m.sb("ones_bf", [P, P], BF16)
        m.upper = m.sb("upper_triangle", [P, P], BF16)
        m.consts = m.sb("consts", [P, E + TILES + BLOCKS])
        m.tmax = m.sb("logit_max", [P, TILES])
        m.tfirst = m.sb("first_choice", [P, TILES])
        m.per_e = m.sb("per_expert", [P, 5, E])
        m.slot_f = m.sb("slots", [P, TILES])
        m.slot_i = m.sb("slot_indices", [P, TILES], mybir.dt.uint32)
        m.block_cmp = m.sb("block_compare", [1, BLOCKS, E])
        m.block_f = m.sb("block_count", [1, BLOCKS])
        m.block_e = m.sb("block_experts", [1, BLOCKS], mybir.dt.int32)
        m.psum_e = m.sb("exp_sums", [P, TILES])
        m.half_p = m.sb("half_probability", [P, TILES])
        m.slots_in = nc.dram_tensor("slots_in", (BLOCKS, P, D), FP32, kind="Internal").ap()
        m.slots_out = nc.dram_tensor("slots_out", (BLOCKS, P, D), FP32, kind="Internal").ap()
        setup_stage(nc, m, x, w_qkv, w_out, cos, sin, consts)
        ffn_stage(nc, m, "ffn1", w1, b1, w2, b2, router)
        project_stage(nc, m)
        attention_stage(nc, m)
        output_stage(nc, m)
        ffn_stage(nc, m, "ffn2", w1, b1, w2, b2, router)
        s_out = m.sem("out_stored")
        with nc.Block() as block:
            @block.sync
            def _(sp):
                sp.dma_start(out.rearrange("b (i p) d -> p b i d", p=P), m.x[:, :, :, :]).then_inc(s_out, 16)
                sp.wait_ge(s_out, 16)


def rope_tables():
    import numpy as np
    half = DH // 2
    inv = (np.float32(1.0) / np.power(np.float32(10000.0), np.arange(half, dtype=np.float32) / np.float32(half))).astype(np.float32)
    ang = (np.arange(L, dtype=np.float32)[:, None] * inv[None, :]).astype(np.float32)
    cos = np.concatenate([np.cos(ang), np.cos(ang)], axis=-1).astype(np.float32).T
    sin = np.concatenate([np.sin(ang), np.sin(ang)], axis=-1).astype(np.float32).T
    return np.tile(cos, (H, 1)), np.tile(sin, (H, 1))


def shape_constants():
    import numpy as np
    row = np.concatenate([np.arange(E, 0, -1), np.arange(TILES) * P, np.arange(BLOCKS)]).astype(np.float32)
    return np.tile(row, (P, 1))


_INS = ["L0_attn_x", "L0_attn_w_qkv", "L0_attn_w_out", "L0_ffn_router_w", "L0_ffn_w1", "L0_ffn_b1", "L0_ffn_w2", "L0_ffn_b2"]


def kernel(**inputs):
    import numpy as _np
    import concourse.bacc as _bacc
    from concourse import mybir as _mybir
    from concourse.bass_utils import run_bass_kernel_spmd as _run

    nc = _bacc.Bacc("TRN2", target_bir_lowering=False, num_devices=1)
    arrays, args = {}, []
    cos, sin = rope_tables()
    given = [(n, inputs[n]) for n in _INS] + [("rope_cos", cos), ("rope_sin", sin), ("shape_constants", shape_constants())]
    for name, a in given:
        a = _np.ascontiguousarray(a)
        arrays[f"in_{name}_dram"] = a
        args.append(nc.dram_tensor(f"in_{name}_dram", a.shape, _mybir.dt.from_np(a.dtype), kind="ExternalInput").ap())
    out = nc.dram_tensor("out_0_dram", (B, L, D), FP32, kind="ExternalOutput").ap()
    program(nc, *args, out)
    r = _run(nc, [arrays], core_ids=[0])
    return r.results[0]["out_0_dram"]
```

```python
import concourse.bass as bass
from concourse import mybir
from contextlib import ExitStack

FP32 = mybir.dt.float32
BF16 = mybir.dt.bfloat16
ALU = mybir.AluOpType
ACT = mybir.ActivationFunctionType
AX = mybir.AxisListType

P = 128
B, L, D = 4, 1024, 128
H, DH = 16, 8
LT = L // P
HALF = 512
NC = L // HALF
GH = 4
NG = H // GH
EPS = 1e-5
SCALE = float(DH) ** -0.5
STACK = 9 * DH
SHIFT = 96
KROWS = SHIFT + 3
SLOTS = 4
E, F = 14, 256
FC = F // P
TILES = B * LT
HT = TILES // 2
RING = 5
HR = -(-(HT + E - 1) // RING)
ROUNDS = 2 * HR
BLOCKS = ROUNDS * RING
HB = BLOCKS // 2
W1, B1 = 0, F
W2 = B1 + FC
B2 = W2 + FC * D
WX = B2 + D
assert HR % 2 == 0
SHARED = 2 * GH * L + B * LT * D + 3 * L


class Memory:

    def __init__(self, nc, ctx):
        self.nc, self.ctx = nc, ctx

    def sb(self, name, shape, dt=FP32):
        return self.ctx.enter_context(self.nc.sbuf_tensor(name, shape, dt))

    def ps(self, name, shape, dt=FP32):
        return self.ctx.enter_context(self.nc.psum_tensor(name, shape, dt))

    def sem(self, name):
        return self.ctx.enter_context(self.nc.semaphore(name))


def over_batches(eng, batch):
    batch(0)
    with eng.Fori(1, B) as b:
        batch(b)


def wait_past(eng, sem, value):
    if not isinstance(value, int) or value > 0:
        eng.wait_ge(sem, value)


def setup_stage(nc, mem, x, w_qkv, w_out, cos, sin, consts):
    m = mem
    s_id = m.sem("identity_made")
    s_ld = m.sem("weights_loaded")
    s_x = m.sem("x_loaded")
    s_tr = m.sem("weights_transposed")
    s_ev = m.sem("weights_copied")
    s_neg = m.sem("weights_rotated")
    s_set = m.sem("constants_set")
    s_zero = m.sem("zeros_made")
    wraw = m.xnT[:, 0:4 * D].rearrange("p (t d) -> p t d", t=4)
    tp = m.st

    with nc.Block() as block:
        @block.sync
        def _(sp):
            sp.dma_start(wraw[:, 0:3, :], w_qkv.rearrange("(t p) d -> p t d", p=P)).then_inc(s_ld, 16)
            sp.dma_start(wraw[:, 3, :], w_out).then_inc(s_ld, 16)
            sp.dma_start(m.cos[:, :], cos).then_inc(s_x, 16)
            sp.dma_start(m.sin[:, :], sin).then_inc(s_x, 16)
            sp.dma_start(m.x[:, :, :, :], x.rearrange("b (i p) d -> p b i d", p=P)).then_inc(s_x, 16)
            sp.dma_start(m.consts[:, :], consts).then_inc(s_x, 16)
            sp.wait_ge(s_zero, 1)
            zeros = m.probs[:, 0:1, 0, 0:D].to_broadcast([P, HB, D])
            for h in range(2):
                sp.dma_start(m.slots_in[h].rearrange("n p d -> p n d"), zeros).then_inc(s_x, 16)
            sp.wait_ge(s_x, 96)

        @block.gpsimd
        def _(pool):
            pool.memset(m.ident[:, :], 0.0).then_inc(s_id, 1)
            pool.wait_ge(s_id, 1)
            pool.affine_select(out=m.ident[:, :], in_=m.ident[:, :], compare_op=ALU.not_equal, fill=1.0,
                               base=0, pattern=[[-1, P]], channel_multiplier=1).then_inc(s_id, 1)
            pool.wait_ge(s_id, 2)
            pool.tensor_copy(m.ident_bf[:, :], m.ident[:, :]).then_inc(s_id, 1)
            for vg in range(2):
                pool.memset(m.vgroup[:, vg, :, :, :], 0.0).then_inc(s_set, 1)
            pool.wait_ge(s_set, 2)
            for vg in range(2):
                pool.memset(m.vgroup[:, vg, :, :, DH:DH + 1], 1.0).then_inc(s_set, 1)
            pool.memset(m.minus_half[:, :], -0.5).then_inc(s_set, 1)
            pool.memset(m.ones_bf[:, :], 1.0).then_inc(s_set, 1)
            pool.wait_ge(s_set, 6)
            pool.affine_select(out=m.upper[:, :], in_=m.ones_bf[:, :], compare_op=ALU.is_ge, fill=0.0,
                               base=0, pattern=[[1, P]], channel_multiplier=-1).then_inc(s_set, 1)
            pool.wait_ge(s_set, 7)
            pool.wait_ge(s_id, 3)

        @block.vector
        def _(dve):
            dve.memset(m.probs[:, 0, 0, 0:D], 0.0).then_inc(s_zero, 1)
            dve.memset(m.ones[:, :], 1.0)
            dve.memset(m.zeros[:, :], 0.0)
            for s in range(4):
                dve.memset(m.qs[64:96, s, :, :], 0.0)
                dve.memset(m.ks[64:96, s, :, :], 0.0)
                last = dve.memset(m.ks[SHIFT:KROWS, s, :, :], 1.0)
            last.then_inc(s_neg, 1)
            dve.wait_ge(s_ev, 1)
            for half, src, sign in ((0, 1, -1.0), (1, 0, 1.0)):
                for n in range(2):
                    o = m.wrT[:, n, :].rearrange("p (h s d) -> p h s d", s=2, d=DH // 2)[:, :, half, :]
                    i = m.wT[:, n, :].rearrange("p (h s d) -> p h s d", s=2, d=DH // 2)[:, :, src, :]
                    last = dve.tensor_scalar(o, i, sign, None, ALU.mult)
            last.then_inc(s_neg, 1)
            dve.wait_ge(s_neg, 2)

        @block.tensor
        def _(pe):
            pe.wait_ge(s_ld, 32)
            pe.wait_ge(s_id, 2)
            for t in range(4):
                last = pe.transpose(tp[0][:, t * P:(t + 1) * P], wraw[:, t, :], m.ident[:, :])
            last.then_inc(s_tr, 1)

        @block.scalar
        def _(act):
            act.wait_ge(s_tr, 1)
            act.activation(m.wT[:, :, :], tp[0][:, :].rearrange("p (t d) -> p t d", t=4), ACT.Copy).then_inc(s_ev, 1)
            act.wait_ge(s_ev, 1)


def layer_norm_stats(dve, m, stats_done, step):
    for t in range(TILES):
        dve.bn_stats(m.stats[:, t, :], m.x[:, t // LT, t % LT, :]).then_inc(stats_done, 1)
    dve.wait_ge(stats_done, TILES)
    mean0, dev0, mean1, dev1 = (m.stats[:, :, n] for n in (1, 2, 4, 5))
    s, d, v, q = (m.ln_tmp[:, n, :] for n in range(4))
    dve.tensor_tensor(s, mean0, mean1, ALU.add).then_inc(step, 1)
    dve.tensor_tensor(d, mean0, mean1, ALU.subtract).then_inc(step, 1)
    dve.tensor_tensor(v, dev0, dev1, ALU.add).then_inc(step, 1)
    dve.wait_ge(step, 2)
    dve.tensor_tensor(q, d, d, ALU.mult).then_inc(step, 1)
    dve.tensor_scalar(m.mean[:, :], s, 0.5, None, ALU.mult).then_inc(step, 1)
    dve.wait_ge(step, 4)
    dve.scalar_tensor_tensor(out=d, in0=q, scalar=D / 4.0, in1=v, op0=ALU.mult, op1=ALU.add).then_inc(step, 1)
    dve.wait_ge(step, 6)
    dve.tensor_scalar(m.veps[:, :], d, 1.0 / D, EPS, ALU.mult, ALU.add).then_inc(step, 1)


def layer_norm_roots(pool, m, step, rstd_done):
    pool.wait_ge(step, 7)
    pool.tensor_tensor(m.rstd[:, :], m.veps[:, :], m.minus_half[:, :], ALU.pow).then_inc(rstd_done, 1)


def normalise(dve, m, b, xn, xn_done):
    for i in range(LT):
        t = b * LT + i
        dve.tensor_scalar(xn[:, i, :], m.x[:, b, i, :], m.mean[:, bass.ds(t, 1)], m.rstd[:, bass.ds(t, 1)],
                          ALU.subtract, ALU.mult).then_inc(xn_done, 1)


def ffn_stage(nc, mem, name, w1, b1, w2, b2, router):
    m = mem
    sem = lambda s: m.sem(f"{name}_{s}")
    stats_done, ln_step = sem("stats_done"), sem("ln_step")
    rstd_done, xn_done = sem("rstd_done"), sem("xn_done")
    router_loaded, bias_loaded, w_loaded = sem("router_loaded"), sem("bias_loaded"), sem("experts_loaded")
    bias_turned, bias_kept = sem("bias_turned"), sem("bias_kept")
    turned, kept = sem("xn_turned"), sem("xnT_kept")
    logits_done = sem("logits_done")
    r = sem("routing_step")
    exped, prefixed, placed = sem("router_exp"), sem("prefixed"), sem("slots_placed")
    scattered = [sem(f"half{h}_scattered") for h in range(2)]
    gathered = [sem(f"rows_gathered{b}") for b in range(B)]
    round_loaded = [sem(f"round{i}_loaded") for i in range(2)]
    round_stored = [sem(f"round{i}_stored") for i in range(2)]
    block_turned, block_kept = sem("block_turned"), sem("block_kept")
    w_copied = sem("block_weights_copied")
    hidden_done, gelu_done = sem("hidden_done"), sem("gelu_done")
    y_done, y_kept = sem("y_done"), sem("y_kept")
    combined = sem("combined")
    CHUNKS = TILES // 4
    CHOICE, SHIFTED, ROUTING = 5, 6, 23
    UP, DOWN = 2, 4

    logits = m.av[0][:, 0:TILES * E].rearrange("p (t e) -> p t e", e=E)
    own = [m.st[0][:, :], m.st[1][:, :], m.mx[0][:, 0:HALF], m.mx[0][:, HALF:], m.mx[1][:, 0:HALF]]
    yb = [m.av[0][:, 0:D], m.av[1][:, 0:D], m.mx[1][:, HALF:HALF + D]]
    yb = [yb[i % 3] for i in range(RING)]
    assert len(own) == RING

    def blocks(eng, step):
        for k in range(2 * RING):
            step(k, k)
        with eng.Fori(1, BLOCKS // (2 * RING)) as it:
            for i in range(2 * RING):
                step(it * 2 * RING + i, i)

    def late(k, n):
        return not isinstance(k, int) or k >= n

    with nc.Block() as block:
        @block.sync
        def _(sp):
            sp.dma_start(m.router[:, :], router).then_inc(router_loaded, 16)
            sp.dma_start(m.b1_rows[:, :], b1.rearrange("e (c p) -> (e c) p", p=P)).then_inc(bias_loaded, 16)
            sp.dma_start(m.wx[:, :, W1:W1 + F], w1.rearrange("e p f -> p e f")).then_inc(w_loaded, 16)
            for c in range(FC):
                sp.dma_start(m.wx[:, :, W2 + c * D:W2 + (c + 1) * D],
                             w2[:, c * P:(c + 1) * P, :].rearrange("e p d -> p e d")).then_inc(w_loaded, 16)
            sp.dma_start(m.wx[:, :, B2:B2 + D], b2.unsqueeze(0).to_broadcast([P, E, D])).then_inc(w_loaded, 16)

            def load(n):
                h, at = n // HR, n % HR * RING
                sp.dma_start(m.xblk[:, n % 2, :, :], m.slots_in[h][at:at + RING, :, :].rearrange("n p d -> p n d"))\
                    .then_inc(round_loaded[n % 2], 16)
            sp.wait_ge(scattered[0], 16 * HT)
            load(0)
            load(1)
            for n in range(ROUNDS):
                if n + 2 < ROUNDS:
                    if n + 2 == HR:
                        sp.wait_ge(scattered[1], 16 * HT)
                    sp.wait_ge(block_turned, RING * (n + 1))
                    load(n + 2)
                sp.wait_ge(y_kept, RING * (n + 1))
                h, at = n // HR, n % HR * RING
                sp.dma_start(m.slots_out[h][at:at + RING, :, :].rearrange("n p d -> p n d"), m.yblk[:, n % 2, :, :])\
                    .then_inc(round_stored[n % 2], 16)
            for i in range(2):
                sp.wait_ge(round_stored[i], 16 * ROUNDS // 2)

        @block.gpsimd
        def _(pool):
            layer_norm_roots(pool, m, ln_step, rstd_done)
            for t in range(TILES):
                if t % HT == 0:
                    pool.wait_ge(placed, t // HT + 1)
                pool.indirect_dma_start(m.slots_in[t // HT].rearrange("n p d -> (n p) d"), bass.IndirectOffsetOnAxis(m.slot_i[:, t:t + 1], 0),
                                        m.rows[:, t // LT, t % LT, :], None).then_inc(scattered[t // HT], 16)
            for t in range(TILES):
                if t % HT == 0:
                    for i in range(2):
                        pool.wait_ge(round_stored[i], 16 * (ROUNDS // 4) * (t // HT + 1))
                pool.indirect_dma_start(m.rows[:, t // LT, t % LT, :], None, m.slots_out[t // HT].rearrange("n p d -> (n p) d"),
                                        bass.IndirectOffsetOnAxis(m.slot_i[:, t:t + 1], 0)).then_inc(gathered[t // LT], 16)

        @block.scalar
        def _(act):
            act.wait_ge(bias_turned, 1)
            act.activation(m.wx[:, :, B1:B1 + FC], m.av[1][:, 0:E * FC].rearrange("p (e c) -> p e c", c=FC),
                           ACT.Copy).then_inc(bias_kept, 1)
            for h in range(2):
                for c in range(h * CHUNKS // 2, (h + 1) * CHUNKS // 2):
                    act.wait_ge(turned, c + 1)
                    wait_past(act, logits_done, c - 3)
                    act.activation(m.fxnT[:, c % 4, :], m.st[c % 2][:, :], ACT.Copy).then_inc(kept, 1)
                act.wait_ge(r, h * ROUTING + SHIFTED)
                ts = slice(h * HT, (h + 1) * HT)
                act.activation(m.rt[3][:, ts, :], m.rt[2][:, ts, :], ACT.Exp).then_inc(exped, 1)

            def gelu(k, i):
                act.wait_ge(hidden_done, k + 1)
                if late(k, RING):
                    act.wait_ge(y_done, k - RING + 1)
                for c in range(FC):
                    last = act.activation(m.hid[:, i, c, :], own[i][:, P * (c + 1):P * (c + 2)], ACT.Gelu,
                                          bias=m.wblk[:, i, B1 + c:B1 + c + 1])
                last.then_inc(gelu_done, 1)

            def step(k, n):
                act.wait_ge(block_turned, k + 1)
                act.activation(m.xT[:, n % RING, :], own[n % RING][:, 0:P], ACT.Copy).then_inc(block_kept, 1)
                if late(k, UP):
                    gelu(k - UP, (n - UP) % RING)
            blocks(act, step)
            for k in range(BLOCKS - UP, BLOCKS):
                gelu(k, k % RING)

        @block.tensor
        def _(pe):
            pe.wait_ge(bias_loaded, 16)
            pe.transpose(m.av[1][:, 0:E * FC], m.b1_rows[:, :], m.ident[0:E * FC, 0:E * FC]).then_inc(bias_turned, 1)
            pe.wait_ge(router_loaded, 16)

            def chunk_logits(c):
                pe.wait_ge(kept, c + 1)
                for t in range(4):
                    last = pe.matmul(logits[:, 4 * c + t, :], m.fxnT[:, c % 4, t * P:(t + 1) * P], m.router[:, :],
                                     start=True, stop=True)
                last.then_inc(logits_done, 1)
            for h in range(2):
                chunks = range(h * CHUNKS // 2, (h + 1) * CHUNKS // 2)
                for c in chunks:
                    pe.wait_ge(xn_done, 4 * c + 4)
                    wait_past(pe, kept, c - 1)
                    for t in range(4):
                        last = pe.transpose(m.st[c % 2][:, t * P:(t + 1) * P], m.rows[:, c * 4 // LT, (4 * c + t) % LT, :],
                                            m.ident[:, :])
                    last.then_inc(turned, 1)
                    if c > chunks[0]:
                        chunk_logits(c - 1)
                chunk_logits(chunks[-1])
                pe.wait_ge(r, h * ROUTING + CHOICE)
                choice = m.choice[:, h * HT:(h + 1) * HT, :].rearrange("p t e -> p (t e)")
                at = h * HT * E
                pe.matmul(m.mx[0][:, at:at + HT * E], m.upper[:, :], choice, start=True, stop=True)
                pe.matmul(m.mx[0][:, HALF + at:HALF + at + HT * E], m.ones_bf[:, :], choice,
                          start=True, stop=True).then_inc(prefixed, 1)

            def turn(k, i, first, n):
                if i == 0:
                    pe.wait_ge(round_loaded[first], 16 * n + 16)
                if late(k, RING):
                    pe.wait_ge(gelu_done, k - RING + 1)
                pe.transpose(own[i][:, 0:P], m.xblk[:, first, i, :], m.ident[:, :]).then_inc(block_turned, 1)

            def up(k, i):
                pe.wait_ge(block_kept, k + 1)
                pe.wait_ge(w_copied, k + 1)
                for c in range(FC):
                    last = pe.matmul(own[i][:, P * (c + 1):P * (c + 2)], m.wblk[:, i, W1 + c * P:W1 + (c + 1) * P],
                                     m.xT[:, i, :], start=True, stop=True)
                last.then_inc(hidden_done, 1)

            def down(k, i):
                pe.wait_ge(gelu_done, k + 1)
                if late(k, 2):
                    pe.wait_ge(y_kept, k - 1)
                for c in range(FC):
                    last = pe.matmul(yb[i], m.hid[:, i, c, :], m.wblk[:, i, W2 + c * D:W2 + (c + 1) * D],
                                     start=(c == 0), stop=(c == FC - 1))
                last.then_inc(y_done, 1)

            def step(k, n):
                turn(k, n % RING, n // RING, k // (2 * RING) if isinstance(k, int) else m.pair[0])
                if late(k, UP):
                    up(k - UP, (n - UP) % RING)
                if late(k, DOWN):
                    down(k - DOWN, (n - DOWN) % RING)
            pe.wait_ge(placed, 2)
            for k in range(2 * RING):
                step(k, k)
            with pe.Fori(1, BLOCKS // (2 * RING)) as it:
                m.pair = [it]
                for i in range(2 * RING):
                    step(it * 2 * RING + i, i)
            for k in range(BLOCKS, BLOCKS + DOWN):
                if k < BLOCKS + UP:
                    up(k - UP, (k - UP) % RING)
                down(k - DOWN, (k - DOWN) % RING)

        @block.vector
        def _(dve):
            layer_norm_stats(dve, m, stats_done, ln_step)
            dve.wait_ge(rstd_done, 1)
            count = [0]

            def routing(make, *args, **kw):
                if count[0]:
                    dve.wait_ge(r, count[0])
                make(*args, **kw).then_inc(r, 1)
                count[0] += 1

            def over_e(a):
                return a.unsqueeze(2).to_broadcast([P, HT, E])

            def over_t(a):
                return a.unsqueeze(1).to_broadcast([P, HT, E])
            flip = lambda a: a.rearrange("p t e -> p (t e)").rearrange("p (e t) -> p e t", e=E)

            def route(h):
                ts, bs = slice(h * HT, (h + 1) * HT), slice(h * HB, (h + 1) * HB)
                T = [a[:, ts, :] for a in m.rt]
                lg, choice = logits[:, ts, :], m.choice[:, ts, :]
                tmax, tfirst = m.tmax[:, ts], m.tfirst[:, ts]
                at = h * HT * E
                prefix = m.mx[0][:, at:at + HT * E].rearrange("p (t e) -> p t e", e=E)
                totals = m.mx[0][:, HALF + at:HALF + at + HT * E].rearrange("p (t e) -> p e t", e=E)
                routing(dve.tensor_reduce, tmax, lg, AX.X, ALU.max)
                routing(dve.tensor_tensor, T[0], lg, over_e(tmax), ALU.is_equal)
                routing(dve.tensor_tensor, T[1], T[0], over_t(m.consts[:, 0:E]), ALU.mult)
                routing(dve.tensor_reduce, tfirst, T[1], AX.X, ALU.max)
                routing(dve.tensor_tensor, choice, over_t(m.consts[:, 0:E]), over_e(tfirst), ALU.is_equal)
                assert count[0] == h * ROUTING + CHOICE
                routing(dve.tensor_tensor, T[2], lg, over_e(tmax), ALU.subtract)
                assert count[0] == h * ROUTING + SHIFTED
                dve.wait_ge(prefixed, h + 1)
                tot, cum, base = flip(T[0]), flip(T[1]), flip(T[4])
                routing(dve.tensor_copy, tot, totals)
                routing(dve.tensor_tensor_scan, cum.rearrange("p e t -> p (e t)"), m.ones[:, 0:HT * E],
                     tot.rearrange("p e t -> p (e t)"), 0.0, ALU.mult, ALU.add)
                cnt, nb, bend, t1, t2 = (m.per_e[:, h, n, :] for n in range(5))
                routing(dve.tensor_reduce, cnt, tot, AX.X, ALU.add)
                routing(dve.tensor_tensor, base, cnt.unsqueeze(2).to_broadcast([P, E, HT]),
                     m.consts[:, E:E + HT].unsqueeze(1).to_broadcast([P, E, HT]), ALU.is_gt)
                routing(dve.tensor_reduce, nb, base, AX.X, ALU.add)
                routing(dve.tensor_tensor_scan, bend, m.ones[:, 0:E], nb, 0.0, ALU.mult, ALU.add)
                routing(dve.tensor_tensor, t1, bend, nb, ALU.subtract)
                routing(dve.scalar_tensor_tensor, out=t2, in0=cum[:, :, HT - 1], scalar=1.0, in1=cnt,
                     op0=ALU.add, op1=ALU.subtract)
                routing(dve.scalar_tensor_tensor, out=t1, in0=t1, scalar=float(P), in1=t2, op0=ALU.mult, op1=ALU.subtract)
                routing(dve.tensor_tensor, cum, cum, tot, ALU.subtract)
                routing(dve.tensor_tensor, base, cum, t1.unsqueeze(2).to_broadcast([P, E, HT]), ALU.add)
                routing(dve.tensor_tensor, T[0], prefix, base.rearrange("p e t -> p t e"), ALU.add)
                routing(dve.tensor_tensor, T[1], T[0], choice, ALU.mult)
                routing(dve.tensor_reduce, m.slot_f[:, ts], T[1], AX.X, ALU.add)
                dve.wait_ge(r, count[0])
                dve.tensor_copy(m.slot_i[:, ts], m.slot_f[:, ts]).then_inc(placed, 1)
                routing(dve.tensor_tensor, m.block_cmp[:, bs, :], bend[0:1, :].unsqueeze(1).to_broadcast([1, HB, E]),
                     m.consts[0:1, E + HT:E + HT + HB].unsqueeze(2).to_broadcast([1, HB, E]), ALU.is_le)
                routing(dve.tensor_reduce, m.block_f[:, bs], m.block_cmp[:, bs, :], AX.X, ALU.add)
                routing(dve.tensor_scalar, m.block_e[:, bs], m.block_f[:, bs], float(E - 1), None, ALU.min)
                assert count[0] == (h + 1) * ROUTING
            for h in range(2):
                for b in range(h * B // 2, (h + 1) * B // 2):
                    normalise(dve, m, b, m.rows[:, b, :, :], xn_done)
                dve.wait_ge(logits_done, (h + 1) * CHUNKS // 2)
                route(h)
            dve.wait_ge(w_loaded, 16 * (2 + FC))
            dve.wait_ge(bias_kept, 1)
            dve.wait_ge(r, count[0])

            def keep(k, n, full):
                dve.wait_ge(y_done, k + 1)
                if full is not None:
                    dve.wait_ge(round_stored[n // RING], full)
                i = n % RING
                dve.tensor_tensor(m.yblk[:, n // RING, i, :], yb[i], m.wblk[:, i, B2:B2 + D], ALU.add).then_inc(y_kept, 1)

            def step(k, n, full):
                if late(k, RING):
                    dve.wait_ge(y_kept, k - RING + 1)
                e = dve.value_load(m.block_e[0:1, bass.ds(k, 1)], min_val=0, max_val=E - 1)
                dve.tensor_copy(m.wblk[:, n % RING, :], m.wx[:, e, :]).then_inc(w_copied, 1)
                if late(k, DOWN):
                    keep(k - DOWN, (n - DOWN) % (2 * RING), full if (n - DOWN) % RING == 0 else None)
            for k in range(2 * RING):
                step(k, k, None)
            with dve.Fori(1, BLOCKS // (2 * RING)) as it:
                for n in range(2 * RING):
                    step(it * 2 * RING + n, n, it * 16)
            for n in range(2 * RING - DOWN, 2 * RING):
                keep(BLOCKS - 2 * RING + n, n, None)
            dve.wait_ge(exped, 2)
            routing(dve.tensor_reduce, m.psum_e[:, :], m.rt[3][:, :, :], AX.X, ALU.add)
            routing(dve.reciprocal, m.tmax[:, :], m.psum_e[:, :])
            routing(dve.tensor_scalar, m.half_p[:, :], m.tmax[:, :], 0.5, None, ALU.mult)
            dve.wait_ge(r, count[0])
            for b in range(B):
                dve.wait_ge(gathered[b], 16 * LT)
                for i in range(LT):
                    t = LT * b + i
                    dve.scalar_tensor_tensor(out=m.x[:, b, i, :], in0=m.rows[:, b, i, :], scalar=m.half_p[:, t:t + 1],
                                             in1=m.x[:, b, i, :], op0=ALU.mult, op1=ALU.add).then_inc(combined, 1)
            dve.wait_ge(combined, TILES)


def project_stage(nc, mem):
    m = mem
    stats_done = m.sem("stats_done")
    ln_step = m.sem("ln_step")
    rstd_done = m.sem("rstd_done")
    xn_done = m.sem("xn_done")
    xn_turned = m.sem("xn_turned")
    xnT_done = m.sem("xnT_done")
    proj_done = m.sem("proj_done")
    v_done = m.sem("v_projected")
    v_kept = m.sem("v_kept")
    scaled = m.sem("rope_products")
    roped = m.sem("roped")
    hi_done = m.sem("hi_done")
    rest1 = m.sem("rest1_done")
    mid_done = m.sem("mid_done")
    lo_done = m.sem("lo_done")
    stored = m.sem("parts_stored")
    STORES = 12 * 16

    banks = [[m.mx[0][:, 0:HALF], m.mx[0][:, HALF:], m.mx[1][:, 0:HALF], m.mx[1][:, HALF:]],
             [m.av[0][:, :], m.av[1][:, :], m.st[0][:, :], m.st[1][:, :]]]

    with nc.Block() as block:
        @block.vector
        def _(dve):
            layer_norm_stats(dve, m, stats_done, ln_step)
            dve.wait_ge(rstd_done, 1)
            def batch(b):
                wait_past(dve, xn_turned, NC * b)
                normalise(dve, m, b, m.xn, xn_done)
                for c in range(NC):
                    dve.wait_ge(proj_done, b * NC + c + 1)
                    wait_past(dve, roped, (b * NC + c) * 2)
                    cs = slice(c * HALF, (c + 1) * HALF)
                    for n in range(2):
                        dve.tensor_tensor(m.tcos[:, n, :], banks[c][2 * n], m.cos[:, cs], ALU.mult).then_inc(scaled, 1)
                        dve.tensor_tensor(m.tsin[:, n, :], banks[c][2 * n + 1], m.sin[:, cs], ALU.mult).then_inc(scaled, 1)
                    for n in range(2):
                        dve.wait_ge(scaled, (b * NC + c) * 4 + 2 * n + 2)
                        wait_past(dve, lo_done, (b * NC + c) * 2)
                        dve.tensor_tensor(m.roped[:, n, :], m.tcos[:, n, :], m.tsin[:, n, :], ALU.add).then_inc(roped, 1)
                for c in range(NC):
                    dve.wait_ge(v_done, b * NC + c + 1)
                    dve.tensor_copy(m.v[:, b, 4 * c:4 * c + 4, :], banks[0][c].rearrange("p (t d) -> p t d", d=D)).then_inc(v_kept, 1)
            over_batches(dve, batch)

        @block.tensor
        def _(pe):
            def batch(b):
                for c in range(NC):
                    pe.wait_ge(xn_done, b * LT + 4 * c + 4)
                    wait_past(pe, scaled, b * 8)
                    for t in range(4):
                        last = pe.transpose(m.st[c][:, t * P:(t + 1) * P], m.xn[:, 4 * c + t, :], m.ident[:, :])
                    last.then_inc(xn_turned, 1)
                for c in range(NC):
                    pe.wait_ge(xnT_done, b * NC + NC)
                    wait_past(pe, v_kept, b * NC)
                    cs = slice(c * HALF, (c + 1) * HALF)
                    for n in range(2):
                        pe.matmul(banks[c][2 * n], m.wT[:, n, :], m.xnT[:, cs], start=True, stop=True)
                        last = pe.matmul(banks[c][2 * n + 1], m.wrT[:, n, :], m.xnT[:, cs], start=True, stop=True)
                    last.then_inc(proj_done, 1)
                pe.wait_ge(scaled, b * 8 + 4)
                for c in range(NC):
                    for t in range(4):
                        i = 4 * c + t
                        last = pe.matmul(banks[0][c][:, t * P:(t + 1) * P], m.xnT[:, i * P:(i + 1) * P], m.wT[:, 2, :],
                                         start=True, stop=True)
                    last.then_inc(v_done, 1)
            over_batches(pe, batch)

        @block.scalar
        def _(act):
            def batch(b):
                for c in range(NC):
                    act.wait_ge(xn_turned, b * NC + c + 1)
                    wait_past(act, v_done, b * NC)
                    act.activation(m.xnT[:, c * HALF:(c + 1) * HALF], m.st[c][:, :], ACT.Copy).then_inc(xnT_done, 1)
                wait_past(act, stored, b * STORES)
                for c in range(NC):
                    cs = slice(c * HALF, (c + 1) * HALF)
                    for n in range(2):
                        k = 2 * c + n + 1
                        act.wait_ge(roped, b * 4 + k)
                        act.activation(m.parts[:, n, 0, cs], m.roped[:, n, :], ACT.Copy).then_inc(hi_done, 1)
                    for n in range(2):
                        k = 2 * c + n + 1
                        act.wait_ge(rest1, b * 4 + k)
                        act.activation(m.parts[:, n, 1, cs], m.rest[:, n, :], ACT.Copy).then_inc(mid_done, 1)
            over_batches(act, batch)

        @block.gpsimd
        def _(pool):
            layer_norm_roots(pool, m, ln_step, rstd_done)
            def batch(b):
                for c in range(NC):
                    cs = slice(c * HALF, (c + 1) * HALF)
                    for n in range(2):
                        k = 2 * c + n + 1
                        pool.wait_ge(hi_done, b * 4 + k)
                        wait_past(pool, lo_done, b * 4 + 2 * c)
                        pool.tensor_tensor(m.rest[:, n, :], m.roped[:, n, :], m.parts[:, n, 0, cs], ALU.subtract).then_inc(rest1, 1)
                    for n in range(2):
                        k = 2 * c + n + 1
                        pool.wait_ge(mid_done, b * 4 + k)
                        pool.tensor_tensor(m.parts[:, n, 2, cs], m.rest[:, n, :], m.parts[:, n, 1, cs], ALU.subtract).then_inc(lo_done, 1)
            over_batches(pool, batch)

        @block.sync
        def _(sp):
            def batch(b):
                sp.wait_ge(lo_done, b * 4 + 4)
                sp.wait_ge(mid_done, b * 4 + 4)
                sp.wait_ge(hi_done, b * 4 + 4)
                for part in range(3):
                    for copy in range(3):
                        sp.dma_start(m.q_store(b, part, copy), m.parts[:, 0, part, :]).then_inc(stored, 16)
                    sp.dma_start(m.k_store(b, part), m.parts[:, 1, part, :]).then_inc(stored, 16)
            over_batches(sp, batch)
            sp.wait_ge(stored, B * STORES)


def attention_stage(nc, mem):
    m = mem
    stack_loaded = [m.sem(f"stack{s}_loaded") for s in range(SLOTS)]
    shift_loaded = [m.sem(f"shift{s}_loaded") for s in range(SLOTS)]
    v_ready = m.sem("v_group_ready")
    turn_full = m.sem("turn_full")
    turn_free = m.sem("turn_free")
    score_full = m.sem("score_full")
    exp_done = m.sem("exp_done")
    pv_done = m.sem("pv_done")
    av_kept = m.sem("av_kept")
    shift_stored = m.sem("shift_stored")
    split = m.sem("shift_split")
    shift_made = m.sem("shift_made")
    shift_turned = m.sem("shift_turned")
    recip_done = m.sem("recip_done")
    ITEMS = GH * LT
    BODY_POS = range(2, LT + 2)
    LATE_POS = 4
    EARLY = ITEMS - 4 * LATE_POS
    BODY = ITEMS + 1
    FIRST = ITEMS + EARLY
    CH = GH * NC
    SHIFT_LOADED = 16 * 3

    def schedule(has_next, has_second):
        out = {p: [] for p in BODY_POS}
        for k, p in enumerate(BODY_POS):
            if k < LATE_POS and has_next:
                out[p] += [("max", 1, EARLY + 4 * k + j) for j in range(4)]
            elif k >= LATE_POS and has_second:
                out[p] += [("max", 2, 4 * (k - LATE_POS) + j) for j in range(4)]
        if has_next:
            out[LATE_POS + 2].insert(2 if has_second else 0, ("shift", 1, 0))
        out[LT + 1].insert(2 if has_second else 0, ("avt", 0, 0))
        return out

    def own_turns(turns):
        return [t for t in turns if t[0] != "shift"]

    def first_turn(b, u):
        short = EARLY if isinstance(b, int) and b == B - 1 and u == NG - 1 else 0
        return FIRST + BODY * (NG * b + u) - short

    def place(b, u, ahead):
        return (b + 1, u + ahead - NG) if u + ahead >= NG else (b, u + ahead)

    def turn_pe(pe, b, u, n, turn, slot):
        kind, ahead, j = turn
        bb, uu = place(b, u, ahead)
        if not isinstance(n, int) or n >= 2:
            pe.wait_ge(turn_free, n - 1)
        out = m.mx[slot]
        if kind == "max":
            h, qt = j // LT, j % LT
            if j == 0:
                pe.wait_ge(stack_loaded[uu], 64 * (bb + 1))
            for c in range(NC):
                last = pe.matmul(out[:, c * HALF:(c + 1) * HALF], m.qs[0:SHIFT, uu, h, qt * P:(qt + 1) * P],
                                 m.ks[0:SHIFT, uu, h, c * HALF:(c + 1) * HALF], start=True, stop=True)
                if c == 0:
                    yield
        else:
            pe.wait_ge(av_kept, 2 * (4 * bb + uu) + 3)
            for qt in range(LT):
                last = pe.transpose(out[:, qt * P:(qt + 1) * P],
                                    m.avs[:, qt // 4, (qt % 4) * P:(qt % 4 + 1) * P], m.ident[:, :])
        last.then_inc(turn_full, 1)

    def turn_dve(dve, b, u, n, turn, slot):
        kind, ahead, j = turn
        bb, uu = place(b, u, ahead)
        g = 4 * bb + uu
        if kind == "shift":
            dve.wait_ge(shift_made, g + 1)
            if not (isinstance(g, int) and g == 0):
                pb, pu = (bb, uu - 1) if uu else (bb - 1, NG - 1)
                dve.wait_ge(shift_loaded[pu], SHIFT_LOADED * (pb + 1))
            dve.transpose(m.m3T[:, :], m.m3[:, :]).then_inc(shift_turned, 1)
            return
        dve.wait_ge(turn_full, n + 1)
        src = m.mx[slot]
        if kind == "max":
            dve.tensor_reduce(m.maxima[:, uu % 2, j:j + 1], src[:, :], AX.X, ALU.max).then_inc(turn_free, 1)
        else:
            t = src[:, :].rearrange("p (q h r) -> p q h r", h=GH, r=32)
            dve.wait_ge(turn_free, n)
            dve.reciprocal(m.recip[:, :, :], t[:, :, :, DH]).then_inc(recip_done, 1)
            dve.wait_ge(recip_done, g + 1)
            o = m.attn[:, bb, :, uu * GH * DH:(uu + 1) * GH * DH].rearrange("p q (h d) -> p q h d", d=DH)
            dve.tensor_tensor(o, t[:, :, :, 0:DH], m.recip[:, :, :].unsqueeze(3).to_broadcast([P, LT, GH, DH]),
                              ALU.mult).then_inc(turn_free, 1)

    def scores(pe, b, u, s, c, h):
        k = CH * (LT * (4 * b + u) + s) + GH * c + h
        if not isinstance(k, int) or k >= 2:
            pe.wait_ge(exp_done, k - 1)
        if s == 0 and c == 0 and h == 0:
            pe.wait_ge(shift_loaded[u], SHIFT_LOADED * (b + 1))
        pe.matmul(m.st[h % 2][:, :], m.ks[0:KROWS, u, h, s * P:(s + 1) * P], m.qs[0:KROWS, u, h, c * HALF:(c + 1) * HALF],
                  start=True, stop=True).then_inc(score_full, 1)

    def product(pe, b, u, s, c):
        g = 4 * b + u
        if s == 0 and c == 0:
            pe.wait_ge(v_ready, g + 1)
            pe.wait_ge(av_kept, 2 * g + 1)
        pe.wait_ge(exp_done, CH * (LT * g + s) + GH * (c + 1))
        for h in range(GH):
            last = pe.matmul(m.av[c][32 * h:32 * h + 32, :], m.vgroup[:, u % 2, s, h, :],
                             m.probs[:, s % 2, h, c * HALF:(c + 1) * HALF], start=(s == 0), stop=(s == LT - 1))
        last.then_inc(pv_done, 1)

    def position_pe(pe, b, u, pos, turns, n, slot, has_next):
        makers = [turn_pe(pe, b, u, n + k, t, (slot + k) % 2) for k, t in enumerate(own_turns(turns))]
        for c in range(NC):
            for what in ("S0", "S1", "V", "S2", "M", "S3", "M", "M", "M"):
                if what == "V":
                    if pos > 0 and (pos <= LT or has_next):
                        product(pe, *step_of(b, u, pos - 1), c)
                elif what[0] == "S":
                    if pos < LT or has_next:
                        scores(pe, *step_of(b, u, pos), c, int(what[1]))
                elif makers:
                    if next(makers[0], "end") == "end":
                        makers.pop(0)
        for t in makers:
            for _ in t:
                pass

    def step_of(b, u, pos):
        return (b, u, pos) if pos < LT else (*place(b, u, 1), pos - LT)

    def body_pe(pe, b, u, has_next, has_second):
        k = 0
        for pos, turns in schedule(has_next, has_second).items():
            position_pe(pe, b, u, pos, turns, first_turn(b, u) + k, first_turn(0, u) + k, has_next)
            k += len(own_turns(turns))

    def body_act(act, b, u, has_next):
        for pos in BODY_POS:
            for c in range(NC):
                if pos < LT or has_next:
                    exps(act, *step_of(b, u, pos), c, range(2))
                if pos == LT:
                    act.wait_ge(pv_done, 2 * (LT * (4 * b + u) + LT - 1) + c + 2)
                    act.activation(m.avs[:, c, :], m.av[c][:, :], ACT.Copy).then_inc(av_kept, 1)
                if pos < LT or has_next:
                    exps(act, *step_of(b, u, pos), c, range(2, GH))

    def exps(act, b, u, s, c, heads):
        for h in heads:
            act.wait_ge(score_full, CH * (LT * (4 * b + u) + s) + GH * c + h + 1)
            act.activation(m.probs[:, s % 2, h, c * HALF:(c + 1) * HALF], m.st[h % 2][:, :], ACT.Exp,
                           scale=SCALE).then_inc(exp_done, 1)

    def first_turns():
        alone = [("max", 0, j) for j in range(ITEMS)] + [("max", 1, j) for j in range(4)] + [("shift", 0, 0)]
        ahead = [("max", 1, j) for j in range(4, EARLY)]
        return [alone, ahead[:6], ahead[6:]]

    def bodies(f):
        def run(eng):
            with eng.Fori(0, B - 1) as b:
                for u in range(NG):
                    f(eng, b, u, True, True)
            for u in range(NG):
                f(eng, B - 1, u, u < NG - 1, u < NG - 2)
        return run

    def load_stack(sp, b, u):
        sp.dma_start(m.qs[0:STACK, u, :, :], m.stack_q(b, u)).then_inc(stack_loaded[u], 16)
        for copy in range(3):
            rows = slice(3 * DH * copy, 3 * DH * (copy + 1))
            sp.dma_start(m.ks[rows, u, :, :], m.stack_k(b, u)).then_inc(stack_loaded[u], 16)

    def load_shift(sp, b, u):
        sp.wait_ge(shift_turned, NG * b + u + 1)
        g = NG * b + u
        sp.dma_start(m.shift_rows[b, u, :, :, :, :].rearrange("a c p r -> (a c) p r"),
                     m.m3T[:, :].rearrange("k (p r) -> k p r", p=3)).then_inc(shift_stored, 16)
        sp.wait_ge(shift_stored, 16 * (g + 1))
        for part in range(3):
            sp.dma_start(m.qs[SHIFT + part:SHIFT + part + 1, u, :, :].rearrange("o h (q a r) -> o (h q) a r", q=LT, a=4),
                         m.shift_rows[b, u, :, :, part:part + 1, :].rearrange("a c o r -> o c a r")).then_inc(shift_loaded[u], 16)

    def last_maximum(b, u):
        if isinstance(b, int) and b == 0 and u == 0:
            return ITEMS - 1
        pb, pu = (b, u - 1) if u else (b - 1, NG - 1)
        return first_turn(pb, pu) + 4 * LATE_POS - 1

    with nc.Block() as block:
        @block.tensor
        def _(pe):
            pe.sem_inc(pv_done, 1)
            alone, *ahead = first_turns()
            for n, turn in enumerate(own_turns(alone)):
                for _ in turn_pe(pe, 0, 0, n, turn, n % 2):
                    pass
            n = len(own_turns(alone))
            for pos, turns in enumerate(ahead):
                position_pe(pe, 0, 0, pos, turns, n, n, True)
                n += len(own_turns(turns))
            bodies(body_pe)(pe)

        @block.vector
        def _(dve):
            n = 0
            for turn in [t for part in first_turns() for t in part]:
                turn_dve(dve, 0, 0, n, turn, n % 2)
                n += len(own_turns([turn]))

            def body(eng, b, u, has_next, has_second):
                k = 0
                for turn in [t for x in schedule(has_next, has_second).values() for t in x]:
                    turn_dve(eng, b, u, first_turn(b, u) + k, turn, (first_turn(0, u) + k) % 2)
                    k += len(own_turns([turn]))
            bodies(body)(dve)

        @block.scalar
        def _(act):
            act.sem_inc(av_kept, 1)
            for s in range(2):
                for c in range(NC):
                    exps(act, 0, 0, s, c, range(GH))
            bodies(lambda eng, b, u, has_next, _: body_act(eng, b, u, has_next))(act)

        @block.gpsimd
        def _(pool):
            def copy_v(b, u):
                pool.tensor_copy(m.vgroup[:, u % 2, :, :, 0:DH],
                                 m.v[:, b, :, u * GH * DH:(u + 1) * GH * DH].rearrange("p t (h d) -> p t h d", d=DH))\
                    .then_inc(v_ready, 1)
            def split_maxima(b, u):
                g = NG * b + u
                mx = m.maxima[:, u % 2, :]
                parts = [m.m3[:, i * ITEMS:(i + 1) * ITEMS] for i in range(3)]
                pool.wait_ge(turn_free, last_maximum(b, u) + 1)
                if not (isinstance(g, int) and g == 0):
                    pool.wait_ge(shift_turned, g)
                pool.tensor_tensor(m.mneg[:, :], m.zeros[:, :], mx, ALU.subtract).then_inc(split, 1)
                pool.wait_ge(split, 4 * g + 1)
                pool.tensor_tensor(parts[0], m.zeros[:, :], mx, ALU.subtract).then_inc(split, 1)
                pool.wait_ge(split, 4 * g + 2)
                pool.tensor_tensor(m.mrest[:, :], m.mneg[:, :], parts[0], ALU.subtract).then_inc(split, 1)
                pool.wait_ge(split, 4 * g + 3)
                pool.tensor_tensor(parts[1], m.zeros[:, :], m.mrest[:, :], ALU.add).then_inc(split, 1)
                pool.wait_ge(split, 4 * g + 4)
                pool.tensor_tensor(parts[2], m.mrest[:, :], parts[1], ALU.subtract).then_inc(shift_made, 1)
            copy_v(0, 0)
            split_maxima(0, 0)

            def body(eng, b, u, has_next, _):
                if has_next:
                    eng.wait_ge(pv_done, 2 * LT * (4 * b + u) + 1)
                    copy_v(*place(b, u, 1))
                    split_maxima(*place(b, u, 1))
            bodies(body)(pool)

        @block.sync
        def _(sp):
            load_stack(sp, 0, 0)
            load_stack(sp, 0, 1)
            load_shift(sp, 0, 0)

            def body(eng, b, u, has_next, has_second):
                if has_second:
                    load_stack(eng, *place(b, u, 2))
                if has_next:
                    load_shift(eng, *place(b, u, 1))
            bodies(body)(sp)
            for s in range(SLOTS):
                sp.wait_ge(shift_loaded[s], SHIFT_LOADED * B)


def output_stage(nc, mem):
    m = mem
    turned = m.sem("attn_turned")
    kept = m.sem("attnT_kept")
    out_done = m.sem("out_projected")
    added = m.sem("x_added")
    with nc.Block() as block:
        @block.tensor
        def _(pe):
            for b in range(B):
                for c in range(NC):
                    wait_past(pe, kept, NC * b)
                    for t in range(4):
                        last = pe.transpose(m.st[c][:, t * P:(t + 1) * P], m.attn[:, b, 4 * c + t, :], m.ident[:, :])
                    last.then_inc(turned, 1)
                for c in range(NC):
                    pe.wait_ge(kept, NC * b + c + 1)
                    wait_past(pe, added, NC * b)
                    for t in range(4):
                        last = pe.matmul(m.av[c][:, t * P:(t + 1) * P], m.xnT[:, (4 * c + t) * P:(4 * c + t + 1) * P],
                                         m.wT[:, 3, :], start=True, stop=True)
                    last.then_inc(out_done, 1)

        @block.scalar
        def _(act):
            for b in range(B):
                for c in range(NC):
                    act.wait_ge(turned, NC * b + c + 1)
                    wait_past(act, out_done, NC * b)
                    act.activation(m.xnT[:, c * HALF:(c + 1) * HALF], m.st[c][:, :], ACT.Copy).then_inc(kept, 1)

        @block.vector
        def _(dve):
            for b in range(B):
                for c in range(NC):
                    dve.wait_ge(out_done, NC * b + c + 1)
                    xs = m.x[:, b, 4 * c:4 * c + 4, :]
                    dve.tensor_tensor(xs, m.av[c][:, :].rearrange("p (t d) -> p t d", d=D), xs, ALU.add).then_inc(added, 1)
            dve.wait_ge(added, NC * B)


def program(nc, x, w_qkv, w_out, router, w1, b1, w2, b2, cos, sin, consts, out):
    with ExitStack() as ctx:
        m = Memory(nc, ctx)
        q_parts = nc.dram_tensor("q_parts", (B, H, STACK, L), BF16, kind="Internal").ap()
        k_parts = nc.dram_tensor("k_parts", (B, H, 3 * DH, L), BF16, kind="Internal").ap()

        m.shift_rows = nc.dram_tensor("shift_rows", (B, NG, 4, GH * LT, 3, 32), BF16, kind="Internal").ap()

        def q_store(b, part, copy):
            r = (3 * part + copy) * DH
            return q_parts[b, :, r:r + DH, :]

        def k_store(b, part):
            return k_parts[b, :, part * DH:(part + 1) * DH, :]

        def stack_q(b, u):
            return q_parts[b, u * GH:(u + 1) * GH, :, :].rearrange("h r t -> r h t")

        def stack_k(b, u):
            return k_parts[b, u * GH:(u + 1) * GH, :, :].rearrange("h r t -> r h t")

        m.q_store, m.k_store, m.stack_q, m.stack_k = q_store, k_store, stack_q, stack_k
        m.x = m.sb("x_tokens", [P, B, LT, D])
        m.ident = m.sb("identity", [P, P])
        m.ident_bf = m.sb("identity_bf", [P, P], BF16)
        m.wT = m.sb("w_transposed", [P, 4, D])
        m.wrT = m.sb("w_rotated", [P, 2, D])
        m.cos = m.sb("rope_cos", [P, L])
        m.sin = m.sb("rope_sin", [P, L])
        m.stats = m.sb("ln_stats", [P, TILES, 6])
        m.ln_tmp = m.sb("ln_steps", [P, 4, TILES])
        m.mean = m.sb("ln_mean", [P, TILES])
        m.veps = m.sb("ln_var_eps", [P, TILES])
        m.rstd = m.sb("ln_rstd", [P, TILES])
        m.minus_half = m.sb("minus_half", [P, TILES])
        scratch = m.sb("scratch", [P, 4 * RING * D])
        m.xnT = scratch[:, 0:L]
        m.avs = scratch[:, L:2 * L].rearrange("p (c t) -> p c t", c=NC)
        m.xblk, m.yblk = (scratch[:, n * 2 * RING * D:(n + 1) * 2 * RING * D].rearrange("p (s r d) -> p s r d", s=2, d=D)
                          for n in range(2))
        m.attn = m.sb("attn_tokens", [P, B, LT, D])
        m.qs = m.sb("q_stacks", [KROWS, SLOTS, GH, L], BF16)
        m.ks = m.sb("k_stacks", [KROWS, SLOTS, GH, L], BF16)
        m.vgroup = m.sb("v_group", [P, 2, LT, GH, 32])
        m.maxima = m.sb("maxima", [P, 2, GH * LT])
        m.mneg = m.sb("maxima_negated", [P, GH * LT])
        m.zeros = m.sb("zeros", [P, GH * LT])
        m.mrest = m.sb("maxima_rest", [P, GH * LT])
        m.m3 = m.sb("maxima_parts", [P, 3 * GH * LT], BF16)
        m.m3T = m.sb("maxima_rows", [P, 3 * GH * LT], BF16)
        m.recip = m.sb("sum_recips", [P, LT, GH])
        m.st = [m.ps(f"scores{i}", [P, HALF]) for i in range(2)]
        m.mx = [m.ps(f"turn{i}", [P, L]) for i in range(2)]
        m.av = [m.ps(f"av{i}", [P, HALF]) for i in range(2)]
        shared = m.sb("shared", [P, SHARED])
        at = [0]

        def take(n):
            at[0] += n
            assert at[0] <= SHARED
            return shared[:, at[0] - n:at[0]]
        m.probs = take(2 * GH * L).rearrange("p (s h t) -> p s h t", s=2, h=GH)
        m.v = take(B * LT * D).rearrange("p (b i d) -> p b i d", b=B, i=LT)
        m.parts = take(3 * L).bitcast(BF16).rearrange("p (n i t) -> p n i t", n=2, i=3)
        m.xn = m.probs[:, 0, 0, :].rearrange("p (i d) -> p i d", d=D)
        m.tcos = m.probs[:, 0, 1, :].rearrange("p (n t) -> p n t", n=2)
        m.tsin = m.probs[:, 0, 2, :].rearrange("p (n t) -> p n t", n=2)
        m.roped = m.probs[:, 0, 3, :].rearrange("p (n t) -> p n t", n=2)
        m.rest = m.probs[:, 1, 0, :].rearrange("p (n t) -> p n t", n=2)
        at[0] = 0
        m.wx = take(E * WX).rearrange("p (e w) -> p e w", e=E)
        m.hid = take(RING * F).rearrange("p (r c t) -> p r c t", r=RING, c=FC)
        m.fxnT = shared[:, at[0]:at[0] + 4 * HALF].rearrange("p (c t) -> p c t", c=4)
        m.wblk = take(RING * WX).rearrange("p (r w) -> p r w", r=RING)
        m.xT = take(RING * P).rearrange("p (r d) -> p r d", r=RING)
        m.rows = m.attn
        m.router = m.sb("router", [P, E])
        m.b1_rows = m.sb("b1_rows", [E * FC, P])
        m.rt = [m.sb(f"routing{i}", [P, TILES, E]) for i in range(5)]
        m.choice = m.sb("choice", [P, TILES, E], BF16)
        m.ones = m.sb("ones", [P, TILES * E])
        m.ones_bf = m.sb("ones_bf", [P, P], BF16)
        m.upper = m.sb("upper_triangle", [P, P], BF16)
        m.consts = m.sb("consts", [P, E + HT + HB])
        m.tmax = m.sb("logit_max", [P, TILES])
        m.tfirst = m.sb("first_choice", [P, TILES])
        m.per_e = m.sb("per_expert", [P, 2, 5, E])
        m.slot_f = m.sb("slots", [P, TILES])
        m.slot_i = m.sb("slot_indices", [P, TILES], mybir.dt.uint32)
        m.block_cmp = m.sb("block_compare", [1, BLOCKS, E])
        m.block_f = m.sb("block_count", [1, BLOCKS])
        m.block_e = m.sb("block_experts", [1, BLOCKS], mybir.dt.int32)
        m.psum_e = m.sb("exp_sums", [P, TILES])
        m.half_p = m.sb("half_probability", [P, TILES])
        m.slots_in, m.slots_out = ([nc.dram_tensor(f"slots_{way}{h}", (HB, P, D), FP32, kind="Internal").ap() for h in range(2)]
                                   for way in ("in", "out"))
        setup_stage(nc, m, x, w_qkv, w_out, cos, sin, consts)
        ffn_stage(nc, m, "ffn1", w1, b1, w2, b2, router)
        project_stage(nc, m)
        attention_stage(nc, m)
        output_stage(nc, m)
        ffn_stage(nc, m, "ffn2", w1, b1, w2, b2, router)
        s_out = m.sem("out_stored")
        with nc.Block() as block:
            @block.sync
            def _(sp):
                sp.dma_start(out.rearrange("b (i p) d -> p b i d", p=P), m.x[:, :, :, :]).then_inc(s_out, 16)
                sp.wait_ge(s_out, 16)


def rope_tables():
    import numpy as np
    half = DH // 2
    inv = (np.float32(1.0) / np.power(np.float32(10000.0), np.arange(half, dtype=np.float32) / np.float32(half))).astype(np.float32)
    ang = (np.arange(L, dtype=np.float32)[:, None] * inv[None, :]).astype(np.float32)
    cos = np.concatenate([np.cos(ang), np.cos(ang)], axis=-1).astype(np.float32).T
    sin = np.concatenate([np.sin(ang), np.sin(ang)], axis=-1).astype(np.float32).T
    return np.tile(cos, (H, 1)), np.tile(sin, (H, 1))


def shape_constants():
    import numpy as np
    row = np.concatenate([np.arange(E, 0, -1), np.arange(HT) * P, np.arange(HB)]).astype(np.float32)
    return np.tile(row, (P, 1))


_INS = ["L0_attn_x", "L0_attn_w_qkv", "L0_attn_w_out", "L0_ffn_router_w", "L0_ffn_w1", "L0_ffn_b1", "L0_ffn_w2", "L0_ffn_b2"]


def kernel(**inputs):
    import numpy as _np
    import concourse.bacc as _bacc
    from concourse import mybir as _mybir
    from concourse.bass_utils import run_bass_kernel_spmd as _run

    nc = _bacc.Bacc("TRN2", target_bir_lowering=False, num_devices=1)
    arrays, args = {}, []
    cos, sin = rope_tables()
    given = [(n, inputs[n]) for n in _INS] + [("rope_cos", cos), ("rope_sin", sin), ("shape_constants", shape_constants())]
    for name, a in given:
        a = _np.ascontiguousarray(a)
        arrays[f"in_{name}_dram"] = a
        args.append(nc.dram_tensor(f"in_{name}_dram", a.shape, _mybir.dt.from_np(a.dtype), kind="ExternalInput").ap())
    out = nc.dram_tensor("out_0_dram", (B, L, D), FP32, kind="ExternalOutput").ap()
    program(nc, *args, out)
    r = _run(nc, [arrays], core_ids=[0])
    return r.results[0]["out_0_dram"]
```

```python
import concourse.bass as bass
from concourse import mybir
from contextlib import ExitStack

FP32 = mybir.dt.float32
BF16 = mybir.dt.bfloat16
ALU = mybir.AluOpType
ACT = mybir.ActivationFunctionType
AX = mybir.AxisListType

P = 128
B, L, D = 4, 1024, 128
H, DH = 16, 8
LT = L // P
HALF = 512
NC = L // HALF
GH = 4
NG = H // GH
EPS = 1e-5
SCALE = float(DH) ** -0.5
STACK = 9 * DH
SHIFT = 96
KROWS = SHIFT + 3
SLOTS = 4
E, F = 14, 256
FC = F // P
TILES = B * LT
HT = TILES // 2
RING = 6
HR = -(-(HT + E - 1) // RING)
ROUNDS = 2 * HR
BLOCKS = ROUNDS * RING
HB = BLOCKS // 2
W1, B1 = 0, F
W2 = B1 + FC
B2 = W2 + FC * D
WX = B2 + D
assert ROUNDS % 2 == 0 and 2 * RING % 4 == 0
STORES = 12 * 16
SHARED = 2 * GH * L + B * LT * D + 3 * L


class Memory:

    def __init__(self, nc, ctx):
        self.nc, self.ctx = nc, ctx

    def sb(self, name, shape, dt=FP32):
        return self.ctx.enter_context(self.nc.sbuf_tensor(name, shape, dt))

    def ps(self, name, shape, dt=FP32):
        return self.ctx.enter_context(self.nc.psum_tensor(name, shape, dt))

    def sem(self, name):
        return self.ctx.enter_context(self.nc.semaphore(name))


def wait_past(eng, sem, value):
    if not isinstance(value, int) or value > 0:
        eng.wait_ge(sem, value)


def setup_stage(nc, mem, x, router, b1, consts):
    m = mem
    id_step = m.sem("identity_made")
    set_step = m.sem("constants_set")
    zeros_set, ones_set = m.sem("zeros_set"), m.sem("ones_set")
    with nc.Block() as block:
        @block.sync
        def _(sp):
            sp.dma_start(m.x[:, 0, :, :], x[0, :, :].rearrange("(i p) d -> p i d", p=P)).then_inc(m.x_loaded[0], 16)
            sp.dma_start(m.router[:, :], router).then_inc(m.router_loaded, 16)
            sp.dma_start(m.b1_rows[:, :], b1.rearrange("e (c p) -> (e c) p", p=P)).then_inc(m.bias_loaded, 16)
            sp.dma_start(m.consts[:, :], consts).then_inc(m.consts_loaded, 16)
            for b in range(1, B):
                sp.dma_start(m.x[:, b, :, :], x[b, :, :].rearrange("(i p) d -> p i d", p=P)).then_inc(m.x_loaded[b], 16)
            sp.wait_ge(zeros_set, 1)
            for h in range(2):
                sp.dma_start(m.slots_in[h].rearrange("n p d -> p n d"), m.zeros[:, :].unsqueeze(1).to_broadcast([P, HB, D]))\
                    .then_inc(m.slots_cleared, 16)

        @block.gpsimd
        def _(pool):
            pool.memset(m.ident[:, :], 0.0).then_inc(id_step, 1)
            pool.memset(m.minus_half[:, :], -0.5).then_inc(set_step, 1)
            pool.memset(m.ones_bf[:, :], 1.0).then_inc(set_step, 1)
            pool.wait_ge(id_step, 1)
            pool.affine_select(out=m.ident[:, :], in_=m.ident[:, :], compare_op=ALU.not_equal, fill=1.0,
                               base=0, pattern=[[-1, P]], channel_multiplier=1).then_inc(id_step, 1)
            pool.wait_ge(set_step, 2)
            pool.affine_select(out=m.upper[:, :], in_=m.ones_bf[:, :], compare_op=ALU.is_ge, fill=0.0,
                               base=0, pattern=[[1, P]], channel_multiplier=-1).then_inc(set_step, 1)
            pool.wait_ge(id_step, 2)
            pool.wait_ge(set_step, 3)

        @block.vector
        def _(dve):
            dve.memset(m.zeros[:, :], 0.0).then_inc(zeros_set, 1)
            dve.memset(m.ones[:, :], 1.0).then_inc(ones_set, 1)
            dve.wait_ge(ones_set, 1)


def attention_loads(sp, m, w_qkv, w_out, cos, sin):
    sp.dma_start(m.wT[:, 0:3, :], w_qkv.rearrange("(t p) d -> p t d", p=P)).then_inc(m.weights_loaded, 16)
    sp.dma_start(m.wT[:, 3, :], w_out).then_inc(m.weights_loaded, 16)
    sp.dma_start(m.cos[:, :], cos).then_inc(m.tables_loaded, 16)
    sp.dma_start(m.sin[:, :], sin).then_inc(m.tables_loaded, 16)
    zeros = m.zeros[STACK:SHIFT, :].bitcast(BF16)
    ones = m.ones_bf[SHIFT:KROWS, :]
    for stack, rows, src in ((m.qs, slice(STACK, SHIFT), zeros), (m.ks, slice(STACK, SHIFT), zeros),
                             (m.ks, slice(SHIFT, KROWS), ones)):
        w = src.shape[1]
        n = SLOTS * GH * L // w
        sp.dma_start(stack[rows, :, :, :].rearrange("r s h (n w) -> r (s h n) w", w=w),
                     src.unsqueeze(1).to_broadcast([src.shape[0], n, w])).then_inc(m.rows_set, 16)


def chunk_stats(dve, m, b, c):
    for i in range(4 * c, 4 * c + 4):
        dve.bn_stats(m.stats[:, b * LT + i, :], m.x[:, b, i, :]).then_inc(m.stats_done, 1)


def layer_norm_step(dve, m, sems, b):
    m.stats_count[0] += LT
    step = sems.ln_step
    ts = slice(b * LT, (b + 1) * LT)
    dve.wait_ge(m.stats_done, m.stats_count[0])
    mean0, dev0, mean1, dev1 = (m.stats[:, ts, n] for n in (1, 2, 4, 5))
    s, d, v, q = (m.ln_tmp[:, n, ts] for n in range(4))
    dve.tensor_tensor(s, mean0, mean1, ALU.add).then_inc(step, 1)
    dve.tensor_tensor(d, mean0, mean1, ALU.subtract).then_inc(step, 1)
    dve.tensor_tensor(v, dev0, dev1, ALU.add).then_inc(step, 1)
    dve.wait_ge(step, 7 * b + 3)
    dve.tensor_tensor(q, d, d, ALU.mult).then_inc(step, 1)
    dve.tensor_scalar(m.mean[:, ts], s, 0.5, None, ALU.mult).then_inc(step, 1)
    dve.wait_ge(step, 7 * b + 5)
    dve.scalar_tensor_tensor(out=d, in0=q, scalar=D / 4.0, in1=v, op0=ALU.mult, op1=ALU.add).then_inc(step, 1)
    dve.wait_ge(step, 7 * b + 6)
    dve.tensor_scalar(m.veps[:, ts], d, 1.0 / D, EPS, ALU.mult, ALU.add).then_inc(step, 1)


def layer_norm_roots(pool, m, sems, b):
    pool.wait_ge(sems.ln_step, 7 * b + 7)
    bs = slice(b * LT, (b + 1) * LT)
    pool.tensor_tensor(m.rstd[:, bs], m.veps[:, bs], m.minus_half[:, bs], ALU.pow).then_inc(sems.rstd_done, 1)


def normalise_tile(dve, m, b, i, xn, xn_done):
    t = b * LT + i
    dve.tensor_scalar(xn, m.x[:, b, i, :], m.mean[:, t:t + 1], m.rstd[:, t:t + 1], ALU.subtract, ALU.mult).then_inc(xn_done, 1)


class LayerNorm:

    def __init__(self, mem):
        self.ln_step = mem.sem("ln_step")
        self.rstd_done = mem.sem("rstd_done")


class Router:
    CHUNKS = TILES // 4
    CHOICE, SHIFTED, ROUTING = 6, 3, 23

    def __init__(self, mem, name):
        sem = lambda s: mem.sem(f"{name}_{s}")
        self.m = mem
        self.ln_step = sem("ln_step")
        self.rstd_done = sem("rstd_done")
        self.xn_done = sem("xn_done")
        self.turned = sem("xn_turned")
        self.kept = sem("xnT_kept")
        self.logits_done = sem("logits_done")
        self.r = sem("routing_step")
        self.exped = sem("router_exp")
        self.prefixed = sem("prefixed")
        self.placed = sem("slots_placed")
        self.scattered = [sem(f"half{h}_scattered") for h in range(2)]
        self.count = [0]
        self.logits = mem.mx[1][:, HALF:HALF + TILES * E].rearrange("p (t e) -> p t e", e=E)
        self.prefix, self.totals = (mem.mx[1][:, n * HT * E:(n + 1) * HT * E] for n in range(2))

    def chunks(self, h):
        return range(h * self.CHUNKS // 2, (h + 1) * self.CHUNKS // 2)

    def normalise(self, dve, b):
        dve.wait_ge(self.rstd_done, b + 1)
        for i in range(LT):
            normalise_tile(dve, self.m, b, i, self.m.rows[:, b, i, :], self.xn_done)

    def turn(self, pe, c, banks):
        m = self.m
        pe.wait_ge(self.xn_done, 4 * c + 4)
        wait_past(pe, self.kept, c - len(banks) + 1)
        for t in range(4):
            last = pe.transpose(banks[c % len(banks)][:, t * P:(t + 1) * P], m.rows[:, c * 4 // LT, (4 * c + t) % LT, :],
                                m.ident[:, :])
        last.then_inc(self.turned, 1)

    def keep(self, copy, eng, c, banks):
        eng.wait_ge(self.turned, c + 1)
        wait_past(eng, self.logits_done, c - 3)
        copy(self.m.fxnT[:, c % 4, :], banks[c % len(banks)]).then_inc(self.kept, 1)

    def project(self, pe, c):
        m = self.m
        pe.wait_ge(self.kept, c + 1)
        for t in range(4):
            last = pe.matmul(self.logits[:, 4 * c + t, :], m.fxnT[:, c % 4, t * P:(t + 1) * P], m.router[:, :],
                             start=True, stop=True)
        last.then_inc(self.logits_done, 1)

    def sum_choices(self, pe, h):
        m = self.m
        pe.wait_ge(self.r, h * self.ROUTING + self.CHOICE)
        choice = m.choice[:, h * HT:(h + 1) * HT, :].rearrange("p t e -> p (t e)")
        pe.matmul(self.prefix, m.upper[:, :], choice, start=True, stop=True)
        pe.matmul(self.totals, m.ones_bf[:, :], choice, start=True, stop=True).then_inc(self.prefixed, 1)

    def exps(self, act, h):
        act.wait_ge(self.r, h * self.ROUTING + self.SHIFTED)
        ts = slice(h * HT, (h + 1) * HT)
        act.activation(self.m.rt[3][:, ts, :], self.m.rt[2][:, ts, :], ACT.Exp).then_inc(self.exped, 1)

    def scatter(self, pool, c):
        m = self.m
        h = c // (self.CHUNKS // 2)
        pool.wait_ge(self.placed, h + 1)
        for t in range(4 * c, 4 * c + 4):
            pool.indirect_dma_start(m.slots_in[h].rearrange("n p d -> (n p) d"), bass.IndirectOffsetOnAxis(m.slot_i[:, t:t + 1], 0),
                                    m.rows[:, t // LT, t % LT, :], None).then_inc(self.scattered[h], 16)

    def step(self, dve, after, make, *args, **kw):
        wait_past(dve, self.r, after)
        make(*args, **kw).then_inc(self.r, 1)
        self.count[0] += 1

    def views(self, h):
        m = self.m
        ts, bs = slice(h * HT, (h + 1) * HT), slice(h * HB, (h + 1) * HB)
        T = [a[:, ts, :] for a in m.rt]
        flip = lambda a: a.rearrange("p t e -> p (t e)").rearrange("p (e t) -> p e t", e=E)
        return ts, bs, T, flip(T[0]), flip(T[1]), flip(T[4]), [m.per_e[:, h, n, :] for n in range(5)]

    def choose(self, dve, h, projected):
        m, first = self.m, h * self.ROUTING
        step = lambda after, make, *args, **kw: self.step(dve, first + after, make, *args, **kw)
        over_e = lambda a: a.unsqueeze(2).to_broadcast([P, HT, E])
        over_t = lambda a: a.unsqueeze(1).to_broadcast([P, HT, E])
        ts, bs, T, tot, cum, base, _ = self.views(h)
        lg, choice, tmax, tfirst = self.logits[:, ts, :], m.choice[:, ts, :], m.tmax[:, ts], m.tfirst[:, ts]
        dve.wait_ge(m.consts_loaded, 16)
        dve.wait_ge(self.logits_done, projected)
        step(0, dve.tensor_reduce, tmax, lg, AX.X, ALU.max)
        step(1, dve.tensor_tensor, T[0], lg, over_e(tmax), ALU.is_equal)
        step(1, dve.tensor_tensor, T[2], lg, over_e(tmax), ALU.subtract)
        assert self.count[0] == first + self.SHIFTED
        step(2, dve.tensor_tensor, T[1], T[0], over_t(m.consts[:, 0:E]), ALU.mult)
        step(4, dve.tensor_reduce, tfirst, T[1], AX.X, ALU.max)
        step(5, dve.tensor_tensor, choice, over_t(m.consts[:, 0:E]), over_e(tfirst), ALU.is_equal)
        assert self.count[0] == first + self.CHOICE

    def divide(self, dve, h):
        m, first = self.m, h * self.ROUTING
        step = lambda after, make, *args, **kw: self.step(dve, first + after, make, *args, **kw)
        ts, bs, T, tot, cum, base, (cnt, nb, bend, t1, t2) = self.views(h)
        totals = self.totals.rearrange("p (t e) -> p e t", e=E)
        dve.wait_ge(self.prefixed, h + 1)
        step(6, dve.tensor_copy, tot, totals)
        step(7, dve.tensor_tensor_scan, cum.rearrange("p e t -> p (e t)"), m.ones[:, 0:HT * E],
             tot.rearrange("p e t -> p (e t)"), 0.0, ALU.mult, ALU.add)
        step(7, dve.tensor_reduce, cnt, tot, AX.X, ALU.add)
        step(9, dve.tensor_tensor, base, cnt.unsqueeze(2).to_broadcast([P, E, HT]),
             m.consts[:, E:E + HT].unsqueeze(1).to_broadcast([P, E, HT]), ALU.is_gt)
        step(9, dve.scalar_tensor_tensor, out=t2, in0=cum[:, :, HT - 1], scalar=1.0, in1=cnt, op0=ALU.add, op1=ALU.subtract)
        step(10, dve.tensor_reduce, nb, base, AX.X, ALU.add)
        step(11, dve.tensor_tensor, cum, cum, tot, ALU.subtract)
        step(12, dve.tensor_tensor_scan, bend, m.ones[:, 0:E], nb, 0.0, ALU.mult, ALU.add)

    def place(self, dve, h):
        m, first = self.m, h * self.ROUTING
        step = lambda after, make, *args, **kw: self.step(dve, first + after, make, *args, **kw)
        ts, bs, T, tot, cum, base, (cnt, nb, bend, t1, t2) = self.views(h)
        prefix = self.prefix.rearrange("p (t e) -> p t e", e=E)
        step(14, dve.tensor_tensor, t1, bend, nb, ALU.subtract)
        step(15, dve.scalar_tensor_tensor, out=t1, in0=t1, scalar=float(P), in1=t2, op0=ALU.mult, op1=ALU.subtract)
        step(16, dve.tensor_tensor, base, cum, t1.unsqueeze(2).to_broadcast([P, E, HT]), ALU.add)
        step(17, dve.tensor_tensor, T[0], prefix, base.rearrange("p e t -> p t e"), ALU.add)
        step(18, dve.tensor_tensor, T[1], T[0], m.choice[:, ts, :], ALU.mult)
        step(19, dve.tensor_reduce, m.slot_f[:, ts], T[1], AX.X, ALU.add)
        dve.wait_ge(self.r, self.count[0])
        dve.tensor_copy(m.slot_i[:, ts], m.slot_f[:, ts]).then_inc(self.placed, 1)
        step(20, dve.tensor_tensor, m.block_cmp[:, :, :], bend[0:1, :].unsqueeze(1).to_broadcast([1, HB, E]),
             m.consts[0:1, E + HT:E + HT + HB].unsqueeze(2).to_broadcast([1, HB, E]), ALU.is_le)
        step(21, dve.tensor_reduce, m.block_f[:, bs], m.block_cmp[:, :, :], AX.X, ALU.add)
        step(22, dve.tensor_scalar, m.block_e[:, :, :].rearrange("o n k -> o (n k)")[:, bs], m.block_f[:, bs],
             float(E - 1), None, ALU.min)
        assert self.count[0] == first + self.ROUTING


def ffn_stage(nc, mem, name, rt, w1, w2, b2, attention=None, norm=None, out=None):
    m = mem
    sem = lambda s: m.sem(f"{name}_{s}")
    halves = range(2) if attention else range(1, 2)
    batches = range(B) if attention else range(B - 1, B)
    chunks_of = lambda h: [c for c in rt.chunks(h) if c // NC in batches]
    w_loaded = sem("experts_loaded")
    bias_turned, bias_kept = sem("bias_turned"), sem("bias_kept")
    out_turned, out_kept = sem("heads_turned"), sem("headsT_kept")
    out_done, out_added = sem("out_projected"), sem("out_added")
    gathered = [sem(f"rows_gathered{c}") for c in range(NC * B)]
    round_loaded = [sem(f"round{i}_loaded") for i in range(2)]
    round_stored = [sem(f"round{i}_stored") for i in range(2)]
    block_turned, block_kept = sem("block_turned"), sem("block_kept")
    w_copied = sem("block_weights_copied")
    hidden_done, gelu_done = sem("hidden_done"), sem("gelu_done")
    y_done, y_kept = sem("y_done"), sem("y_kept")
    combined = sem("combined")
    w_turned, w_kept, w_rotated = sem("weights_transposed"), sem("weights_copied"), sem("weights_rotated")
    UP, DOWN = 2, 4

    gathered_halves, combines = (1, NC) if attention else (2, NC * B)
    v_set = sem("v_groups_set")

    def gather(pool, q):
        for t in range(4 * q, 4 * q + 4):
            pool.indirect_dma_start(m.rows[:, t // LT, t % LT, :], None, m.slots_out[t // HT].rearrange("n p d -> (n p) d"),
                                    bass.IndirectOffsetOnAxis(m.slot_i[:, t:t + 1], 0)).then_inc(gathered[q], 16)

    def combine(dve, q):
        b, c = q // NC, q % NC
        dve.wait_ge(gathered[q], 16 * 4)
        for i in range(4 * c, 4 * c + 4):
            t = LT * b + i
            dve.scalar_tensor_tensor(out=m.x[:, b, i, :], in0=m.rows[:, b, i, :], scalar=m.half_p[:, t:t + 1],
                                     in1=m.x[:, b, i, :], op0=ALU.mult, op1=ALU.add).then_inc(combined, 1)
        if attention:
            dve.wait_ge(combined, 4 * (q + 1))
            chunk_stats(dve, m, b, c)
            if c == NC - 1:
                layer_norm_step(dve, m, norm, b)

    turn_banks = [m.st[0][:, :], m.st[1][:, :]]
    own = [m.st[0][:, :], m.st[1][:, :]] + [m.mx[i][:, j * HALF:(j + 1) * HALF] for i in range(2) for j in range(2)]
    yb = [m.av[i % 2][:, 0:D] for i in range(RING)]
    assert len(own) == RING

    def blocks(eng, step):
        for k in range(2 * RING):
            step(k, k)
        with eng.Fori(1, BLOCKS // (2 * RING)) as it:
            for i in range(2 * RING):
                step(it * 2 * RING + i, i)

    def late(k, n):
        return not isinstance(k, int) or k >= n

    with nc.Block() as block:
        @block.sync
        def _(sp):
            sp.dma_start(m.wx[:, :, W1:W1 + F], w1.rearrange("e p f -> p e f")).then_inc(w_loaded, 16)
            for c in range(FC):
                sp.dma_start(m.wx[:, :, W2 + c * D:W2 + (c + 1) * D],
                             w2[:, c * P:(c + 1) * P, :].rearrange("e p d -> p e d")).then_inc(w_loaded, 16)
            sp.dma_start(m.wx[:, :, B2:B2 + D], b2.unsqueeze(0).to_broadcast([P, E, D])).then_inc(w_loaded, 16)

            if attention:
                attention_loads(sp, m, *attention)

            def load(n):
                h, at = n // HR, n % HR * RING
                sp.dma_start(m.xblk[:, n % 2, :, :], m.slots_in[h][at:at + RING, :, :].rearrange("n p d -> p n d"))\
                    .then_inc(round_loaded[n % 2], 16)
            if not attention:
                sp.wait_ge(out_done, NC)
            sp.wait_ge(rt.scattered[0], 16 * HT)
            load(0)
            load(1)
            for n in range(ROUNDS):
                if n + 2 < ROUNDS:
                    if n + 2 == HR:
                        sp.wait_ge(rt.scattered[1], 16 * HT)
                    sp.wait_ge(block_turned, RING * (n + 1))
                    load(n + 2)
                sp.wait_ge(y_kept, RING * (n + 1))
                h, at = n // HR, n % HR * RING
                sp.dma_start(m.slots_out[h][at:at + RING, :, :].rearrange("n p d -> p n d"), m.yblk[:, n % 2, :, :])\
                    .then_inc(round_stored[n % 2], 16)
            for i in range(2):
                sp.wait_ge(round_stored[i], 16 * ROUNDS // 2)
            if out is not None:
                for b in range(B):
                    sp.wait_ge(combined, LT * (b + 1))
                    sp.dma_start(out[b, :, :].rearrange("(i p) d -> p i d", p=P), m.x[:, b, :, :]).then_inc(m.out_stored, 16)
                sp.wait_ge(m.out_stored, 16 * B)

        @block.gpsimd
        def _(pool):
            if attention:
                for b in range(B):
                    layer_norm_roots(pool, m, rt, b)
            pool.wait_ge(m.slots_cleared, 32)
            for c in range(rt.CHUNKS):
                rt.scatter(pool, c)
                if c == 0 and not attention:
                    layer_norm_roots(pool, m, rt, B - 1)
            if attention:
                for vg in range(2):
                    pool.memset(m.vgroup[:, vg, :, :, :], 0.0).then_inc(v_set, 1)
                pool.wait_ge(v_set, 2)
                for vg in range(2):
                    pool.memset(m.vgroup[:, vg, :, :, DH:DH + 1], 1.0).then_inc(v_set, 1)
                pool.wait_ge(v_set, 4)
            for h in range(gathered_halves):
                rounds = HR * (h + 1)
                pool.wait_ge(round_stored[0], 16 * ((rounds + 1) // 2))
                pool.wait_ge(round_stored[1], 16 * (rounds // 2))
                for q in rt.chunks(h):
                    gather(pool, q)
            if attention:
                layer_norm_roots(pool, m, norm, 0)

        @block.scalar
        def _(act):
            act.wait_ge(bias_turned, 1)
            act.activation(m.wx[:, :, B1:B1 + FC], m.av[1][:, 0:E * FC].rearrange("p (e c) -> p e c", c=FC),
                           ACT.Copy).then_inc(bias_kept, 1)
            if not attention:
                for c in range(NC):
                    act.wait_ge(out_turned, c + 1)
                    act.activation(m.pxnT[c][:, :], m.st[c][:, :], ACT.Copy).then_inc(out_kept, 1)
            for h in halves:
                for c in chunks_of(h):
                    rt.keep(lambda o, i: act.activation(o, i, ACT.Copy), act, c, turn_banks)
                rt.exps(act, h)

            def gelu(k, i):
                act.wait_ge(hidden_done, k + 1)
                if late(k, RING):
                    act.wait_ge(y_done, k - RING + 1)
                for c in range(FC):
                    last = act.activation(m.hid[:, i, c, :], own[i][:, P * (c + 1):P * (c + 2)], ACT.Gelu,
                                          bias=m.wblk[:, i, B1 + c:B1 + c + 1])
                last.then_inc(gelu_done, 1)

            def step(k, n):
                act.wait_ge(block_turned, k + 1)
                act.activation(m.xT[:, n % RING, :], own[n % RING][:, 0:P], ACT.Copy).then_inc(block_kept, 1)
                if late(k, UP):
                    gelu(k - UP, (n - UP) % RING)
            blocks(act, step)
            for k in range(BLOCKS - UP, BLOCKS):
                gelu(k, k % RING)
            if attention:
                act.wait_ge(w_turned, 1)
                act.activation(m.wT[:, :, :], m.st[0][:, :].rearrange("p (t d) -> p t d", t=4), ACT.Copy).then_inc(w_kept, 1)
                act.wait_ge(w_kept, 1)
                for half, src, sign in ((0, 1, -1.0), (1, 0, 1.0)):
                    for n in range(2):
                        o = m.wrT[:, n, :].rearrange("p (h s d) -> p h s d", s=2, d=DH // 2)[:, :, half, :]
                        i = m.wT[:, n, :].rearrange("p (h s d) -> p h s d", s=2, d=DH // 2)[:, :, src, :]
                        act.activation(o, i, ACT.Copy, scale=sign).then_inc(w_rotated, 1)

        @block.tensor
        def _(pe):
            pe.wait_ge(m.bias_loaded, 16)
            pe.transpose(m.av[1][:, 0:E * FC], m.b1_rows[:, :], m.ident[0:E * FC, 0:E * FC]).then_inc(bias_turned, 1)
            pe.wait_ge(m.router_loaded, 16)

            if not attention:
                for c in range(NC):
                    for t in range(4):
                        last = pe.transpose(m.st[c][:, t * P:(t + 1) * P], m.attn[:, B - 1, 4 * c + t, :], m.ident[:, :])
                    last.then_inc(out_turned, 1)
                for c in range(NC):
                    pe.wait_ge(out_kept, c + 1)
                    for t in range(4):
                        last = pe.matmul(m.av[0][:, t * P:(t + 1) * P] if c == 0 else m.mx[0][:, t * P:(t + 1) * P],
                                         m.pxnT[c][:, t * P:(t + 1) * P], m.wT[:, 3, :], start=True, stop=True)
                    last.then_inc(out_done, 1)
            for h in halves:
                chunks = chunks_of(h)
                for c in chunks:
                    rt.turn(pe, c, turn_banks)
                    if c > chunks[0]:
                        rt.project(pe, c - 1)
                rt.project(pe, chunks[-1])
                rt.sum_choices(pe, h)

            def turn(k, i, first, n):
                if i == 0:
                    pe.wait_ge(round_loaded[first], 16 * n + 16)
                if late(k, RING):
                    pe.wait_ge(gelu_done, k - RING + 1)
                pe.transpose(own[i][:, 0:P], m.xblk[:, first, i, :], m.ident[:, :]).then_inc(block_turned, 1)

            def up(k, i):
                pe.wait_ge(block_kept, k + 1)
                pe.wait_ge(w_copied, k + 1)
                for c in range(FC):
                    last = pe.matmul(own[i][:, P * (c + 1):P * (c + 2)], m.wblk[:, i, W1 + c * P:W1 + (c + 1) * P],
                                     m.xT[:, i, :], start=True, stop=True)
                last.then_inc(hidden_done, 1)

            def down(k, i):
                pe.wait_ge(gelu_done, k + 1)
                if late(k, 2):
                    pe.wait_ge(y_kept, k - 1)
                for c in range(FC):
                    last = pe.matmul(yb[i], m.hid[:, i, c, :], m.wblk[:, i, W2 + c * D:W2 + (c + 1) * D],
                                     start=(c == 0), stop=(c == FC - 1))
                last.then_inc(y_done, 1)

            def step(k, n, pair):
                turn(k, n % RING, n // RING, pair)
                if late(k, UP):
                    up(k - UP, (n - UP) % RING)
                if late(k, DOWN):
                    down(k - DOWN, (n - DOWN) % RING)
            pe.wait_ge(rt.placed, 2)
            for k in range(2 * RING):
                step(k, k, 0)
            with pe.Fori(1, BLOCKS // (2 * RING)) as it:
                for i in range(2 * RING):
                    step(it * 2 * RING + i, i, it)
            for k in range(BLOCKS, BLOCKS + DOWN):
                if k < BLOCKS + UP:
                    up(k - UP, (k - UP) % RING)
                down(k - DOWN, (k - DOWN) % RING)
            if attention:
                pe.wait_ge(m.weights_loaded, 32)
                for t in range(4):
                    last = pe.transpose(m.st[0][:, t * P:(t + 1) * P], m.wT[:, t, :], m.ident[:, :])
                last.then_inc(w_turned, 1)

        @block.vector
        def _(dve):
            if not attention:
                rt.place(dve, 0)
                for c in range(NC):
                    dve.wait_ge(out_done, c + 1)
                    xs = m.x[:, B - 1, 4 * c:4 * c + 4, :]
                    src = (m.av[0][:, :], m.mx[0][:, 0:HALF])[c]
                    dve.tensor_tensor(xs, src.rearrange("p (t d) -> p t d", d=D), xs, ALU.add).then_inc(out_added, 1)
                    dve.wait_ge(out_added, c + 1)
                    chunk_stats(dve, m, B - 1, c)
            if attention:
                def stats(b):
                    dve.wait_ge(m.x_loaded[b], 16)
                    for c in range(NC):
                        chunk_stats(dve, m, b, c)
                    layer_norm_step(dve, m, rt, b)
                stats(0)
                stats(1)
                for b in range(2):
                    rt.normalise(dve, b)
                    stats(b + 2)
                rt.normalise(dve, 2)
                rt.normalise(dve, 3)
                rt.choose(dve, 0, rt.CHUNKS // 2)
                rt.divide(dve, 0)
                rt.place(dve, 0)
            else:
                layer_norm_step(dve, m, rt, B - 1)
                rt.normalise(dve, B - 1)
            rt.choose(dve, 1, rt.CHUNKS)
            rt.divide(dve, 1)
            rt.place(dve, 1)
            dve.wait_ge(w_loaded, 16 * (2 + FC))
            dve.wait_ge(bias_kept, 1)
            dve.wait_ge(rt.r, rt.count[0])

            def keep(k, n, full):
                dve.wait_ge(y_done, k + 1)
                if full is not None:
                    dve.wait_ge(round_stored[n // RING], full)
                i = n % RING
                dve.tensor_tensor(m.yblk[:, n // RING, i, :], yb[i], m.wblk[:, i, B2:B2 + D], ALU.add).then_inc(y_kept, 1)

            def load_experts(pair, n):
                _, experts[n:n + 4] = nc.values_load_multi_w_load_instructions(
                    m.block_e[0:1, pair, n:n + 4], engines=[mybir.EngineType.DVE], min_val=0, max_val=E - 1,
                    skip_runtime_bounds_check_because="the routing counts experts up to E and takes the least of that and E - 1")
            experts = [None] * (2 * RING)

            def step(k, n, full):
                if late(k, RING):
                    dve.wait_ge(y_kept, k - RING + 1)
                dve.tensor_copy(m.wblk[:, n % RING, :], m.wx[:, experts[n], :]).then_inc(w_copied, 1)
                if late(k, DOWN):
                    keep(k - DOWN, (n - DOWN) % (2 * RING), full if (n - DOWN) % RING == 0 else None)
            for k in range(2 * RING):
                if k % 4 == 0:
                    load_experts(0, k)
                step(k, k, None)
            with dve.Fori(1, BLOCKS // (2 * RING)) as it:
                for n in range(2 * RING):
                    if n % 4 == 0:
                        load_experts(it, n)
                    step(it * 2 * RING + n, n, it * 16)
            dve.wait_ge(rt.exped, 2)
            rt.step(dve, rt.count[0], dve.tensor_reduce, m.psum_e[:, :], m.rt[3][:, :, :], AX.X, ALU.add)
            rt.step(dve, rt.count[0], dve.reciprocal, m.tmax[:, :], m.psum_e[:, :])
            rt.step(dve, rt.count[0], dve.tensor_scalar, m.half_p[:, :], m.tmax[:, :], 0.5, None, ALU.mult)
            for n in range(2 * RING - DOWN, 2 * RING):
                keep(BLOCKS - 2 * RING + n, n, None)
            dve.wait_ge(rt.r, rt.count[0])
            for q in range(combines):
                combine(dve, q)
    return gather, combine, combined


def project_stage(nc, mem, norm, gather, combine, combined):
    m = mem

    rstd_done = norm.rstd_done
    shift_done = m.sem("norm_shift_done")
    xn_done = m.sem("xn_done")
    xn_turned = m.sem("xn_turned")
    xnT_done = m.sem("xnT_done")
    proj_done = m.sem("proj_done")
    v_done = m.sem("v_projected")
    v_kept = m.sem("v_kept")
    scaled = m.sem("rope_products")
    roped = m.sem("roped")
    hi_done = m.sem("hi_done")
    rest1 = m.sem("rest1_done")
    mid_done = m.sem("mid_done")
    lo_done = m.sem("lo_done")
    klo_done = m.sem("k_lo_done")
    stored = m.parts_stored

    def third(eng, q, n, done):
        b, c = q // NC, q % NC
        cs = slice(c * HALF, (c + 1) * HALF)
        eng.tensor_tensor(m.parts[b % 2][:, n, 2, cs], m.rest[c][:, n, :], m.parts[b % 2][:, n, 1, cs],
                          ALU.subtract).then_inc(done, 1)

    def second(act, q):
        b, c = q // NC, q % NC
        for n in range(2):
            act.wait_ge(rest1, 2 * q + n + 1)
            act.activation(m.parts[b % 2][:, n, 1, c * HALF:(c + 1) * HALF], m.rest[c][:, n, :],
                           ACT.Copy).then_inc(mid_done, 1)

    def rests(pool, q):
        b, c = q // NC, q % NC
        for n in range(2):
            pool.wait_ge(hi_done, 2 * q + n + 1)
            wait_past(pool, (lo_done, klo_done)[n], q - 1)
            pool.tensor_tensor(m.rest[c][:, n, :], m.roped[c][:, n, :], m.parts[b % 2][:, n, 0, c * HALF:(c + 1) * HALF],
                               ALU.subtract).then_inc(rest1, 1)

    def store_batch(sp, b):
        for part in range(3):
            if part < 2:
                sp.wait_ge((hi_done, mid_done)[part], 4 * b + 4)
            else:
                sp.wait_ge(lo_done, 2 * b + 2)
                sp.wait_ge(klo_done, 2 * b + 2)
            store_part(sp, m, b, part)

    pairs = [(m.mx[n][:, 0:HALF], m.mx[n][:, HALF:]) for n in range(2)]

    with nc.Block() as block:
        @block.vector
        def _(dve):
            def shift(b):
                dve.wait_ge(rstd_done, b + 1)
                bs = slice(b * LT, (b + 1) * LT)
                dve.scalar_tensor_tensor(out=m.shift[:, bs], in0=m.mean[:, bs], scalar=-1.0, in1=m.rstd[:, bs],
                                         op0=ALU.mult, op1=ALU.mult).then_inc(shift_done, 1)
            shift(0)
            for q in range(NC, 2 * NC):
                combine(dve, q)
            shift(1)
            dve.wait_ge(m.tables_loaded, 32)

            for q in range(NC * B):
                b, c = q // NC, q % NC
                for n in range(2):
                    dve.wait_ge(proj_done, 2 * q + n + 1)
                    wait_past(dve, roped, 2 * (q - 2) + n + 1)
                    cs = slice(c * HALF, (c + 1) * HALF)
                    dve.tensor_tensor(m.tcos[c][:, n, :], pairs[n][0], m.cos[:, cs], ALU.mult).then_inc(scaled, 1)
                    dve.tensor_tensor(m.tsin[c][:, n, :], pairs[n][1], m.sin[:, cs], ALU.mult).then_inc(scaled, 1)
                for n in range(2):
                    dve.wait_ge(scaled, 4 * q + 2 * n + 2)
                    wait_past(dve, rest1, 2 * (q - 2) + n + 1)
                    dve.tensor_tensor(m.roped[c][:, n, :], m.tcos[c][:, n, :], m.tsin[c][:, n, :], ALU.add).then_inc(roped, 1)
                if q == 1:
                    shift(2)
                if q < 2:
                    for later in range(NC * (q + 2), NC * (q + 3)):
                        combine(dve, later)
                if q == 2:
                    shift(3)
                if q > 0:
                    dve.wait_ge(mid_done, 2 * q)
                    third(dve, q - 1, 1, klo_done)

        @block.tensor
        def _(pe):
            def turn(q):
                b, c = q // NC, q % NC
                pe.wait_ge(xn_done, 4 * q + 4)
                wait_past(pe, xnT_done, q - 1)
                for t in range(4):
                    last = pe.transpose(m.st[c][:, t * P:(t + 1) * P], m.xn[b % 2][:, 4 * c + t, :], m.ident[:, :])
                last.then_inc(xn_turned, 1)

            def pair(q, n):
                wait_past(pe, scaled, 4 * (q - 1) + 2 * n + 2)
                x = m.pxnT[q % 2][:, :]
                pe.matmul(pairs[n][0], m.wT[:, n, :], x, start=True, stop=True)
                pe.matmul(pairs[n][1], m.wrT[:, n, :], x, start=True, stop=True).then_inc(proj_done, 1)
            turn(0)
            for q in range(NC * B):
                pe.wait_ge(xnT_done, q + 1)
                pair(q, 0)
                if q + 1 < NC * B:
                    turn(q + 1)
                pair(q, 1)
                wait_past(pe, v_kept, q - 1)
                for t in range(4):
                    last = pe.matmul(m.av[q % 2][:, t * P:(t + 1) * P], m.pxnT[q % 2][:, t * P:(t + 1) * P], m.wT[:, 2, :],
                                     start=True, stop=True)
                last.then_inc(v_done, 1)

        @block.scalar
        def _(act):
            def chunk_norm(q):
                b = q // NC
                act.wait_ge(shift_done, b + 1)
                wait_past(act, xn_turned, q - 3)
                for i in range(q % NC * 4, q % NC * 4 + 4):
                    t = b * LT + i
                    act.activation(m.xn[b % 2][:, i, :], m.x[:, b, i, :], ACT.Identity, bias=m.shift[:, t:t + 1],
                                   scale=m.rstd[:, t:t + 1]).then_inc(xn_done, 1)

            def keep(q):
                act.wait_ge(xn_turned, q + 1)
                wait_past(act, v_done, q - 1)
                act.activation(m.pxnT[q % 2][:, :], m.st[q % 2][:, :], ACT.Copy).then_inc(xnT_done, 1)
            chunk_norm(0)
            chunk_norm(1)
            keep(0)
            for q in range(NC * B):
                b, c = q // NC, q % NC
                cs = slice(c * HALF, (c + 1) * HALF)
                if q + 1 < NC * B:
                    keep(q + 1)
                if q + 2 < NC * B:
                    chunk_norm(q + 2)
                if q > 0:
                    second(act, q - 1)
                if q == NC:
                    act.wait_ge(combined, TILES)
                if c == 0:
                    wait_past(act, stored[b % 2], b // 2 * STORES)
                for n in range(2):
                    act.wait_ge(roped, 2 * q + n + 1)
                    act.activation(m.parts[b % 2][:, n, 0, cs], m.roped[c][:, n, :], ACT.Copy).then_inc(hi_done, 1)
                act.wait_ge(v_done, q + 1)
                act.activation(m.v[:, b, 4 * c:4 * c + 4, :], m.av[q % 2][:, :].rearrange("p (t d) -> p t d", d=D),
                               ACT.Copy).then_inc(v_kept, 1)

        @block.gpsimd
        def _(pool):
            gather(pool, 4)
            layer_norm_roots(pool, m, norm, 1)
            for q in range(5, NC * B):
                gather(pool, q)
            layer_norm_roots(pool, m, norm, 2)
            for q in range(NC * B - 1):
                rests(pool, q)
                if q == 0:
                    layer_norm_roots(pool, m, norm, 3)
                if q > 0:
                    pool.wait_ge(mid_done, 2 * q - 1)
                    third(pool, q - 1, 0, lo_done)

        @block.sync
        def _(sp):
            store_batch(sp, 0)
            store_batch(sp, 1)
            sp.wait_ge(stored[0], STORES)
            sp.wait_ge(m.rows_set, 48)
            for u in range(2):
                load_stack(sp, m, 0, u)

    last = NC * B - 1

    def finish_act(act):
        second(act, last)

    def finish_pool(pool):
        rests(pool, last)
        pool.wait_ge(mid_done, 2 * last - 1)
        third(pool, last - 1, 0, lo_done)
        for n in range(2):
            pool.wait_ge(mid_done, 2 * last + n + 1)
            third(pool, last, n, (lo_done, klo_done)[n])

    def finish_sp(sp):
        for b in range(2, B):
            store_batch(sp, b)
        for i in range(2):
            sp.wait_ge(m.parts_stored[i], B // 2 * STORES)
    return finish_act, finish_pool, finish_sp


def store_part(sp, m, b, part):
    for copy in range(3):
        sp.dma_start(m.q_store(b, part, copy), m.parts[b % 2][:, 0, part, :]).then_inc(m.parts_stored[b % 2], 16)
    sp.dma_start(m.k_store(b, part), m.parts[b % 2][:, 1, part, :]).then_inc(m.parts_stored[b % 2], 16)


def load_stack(sp, m, b, u):
    sp.dma_start(m.qs[0:STACK, u, :, :], m.stack_q(b, u)).then_inc(m.stack_loaded[u], 16)
    for copy in range(3):
        rows = slice(3 * DH * copy, 3 * DH * (copy + 1))
        sp.dma_start(m.ks[rows, u, :, :], m.stack_k(b, u)).then_inc(m.stack_loaded[u], 16)


def attention_stage(nc, mem, rt, last_parts):
    m = mem
    shift_loaded = [m.sem(f"shift{s}_loaded") for s in range(SLOTS)]
    v_ready = m.sem("v_group_ready")
    turn_full = m.sem("turn_full")
    turn_free = m.sem("turn_free")
    score_full = m.sem("score_full")
    exp_done = m.sem("exp_done")
    pv_done = m.sem("pv_done")
    av_kept = m.sem("av_kept")
    shift_stored = m.sem("shift_stored")
    split = m.sem("shift_split")
    shift_made = m.sem("shift_made")
    shift_turned = m.sem("shift_turned")
    recip_done = m.sem("recip_done")
    finish_act, finish_pool, finish_sp = last_parts
    ITEMS = GH * LT
    BODY_POS = range(2, LT + 2)
    LATE_POS = 4
    EARLY = ITEMS - 4 * LATE_POS
    BODY = ITEMS + 1
    FIRST = ITEMS + EARLY
    WIDE_FROM = 2
    CH = GH * NC
    SHIFT_LOADED = 16 * 3

    ROUTES = {(4, 1): [("turn", 0)], (5, 0): [("turn", 1), ("project", 0)], (5, 1): [("turn", 2), ("project", 1)],
              (6, 0): [("turn", 3), ("project", 2)], (6, 1): [("turn", 4), ("project", 3)],
              (7, 0): [("turn", 5), ("project", 4)], (7, 1): [("project", 5)], (8, 0): [("sum", None)]}
    route_bank = [m.mx[1][:, 0:HALF]]

    def schedule(has_next, has_second):
        out = {p: [] for p in BODY_POS}
        for k, p in enumerate(BODY_POS):
            if k < LATE_POS and has_next:
                out[p] += [("max", 1, EARLY + 4 * k + j) for j in range(4)]
            elif k >= LATE_POS and has_second:
                out[p] += [("max", 2, 4 * (k - LATE_POS) + j) for j in range(4)]
        if has_next:
            out[LATE_POS + 2].insert(2 if has_second else 0, ("shift", 1, 0))
        out[LT + 1].insert(2 if has_second else 0, ("avt", 0, 0))
        if has_next and not has_second:
            rest = [("heads" if k < NC else "out", 0, (b, k % NC)) for b in range(B - 1) for k in range(2 * NC)]
            for k, p in enumerate(range(LT - 2, LT + 2)):
                out[p] += rest[k * len(rest) // 4:(k + 1) * len(rest) // 4]
        return out

    def own_turns(turns):
        return [t for t in turns if t[0] != "shift"]

    def first_turn(b, u):
        short = EARLY - 2 * NC * (B - 1) if isinstance(b, int) and b == B - 1 and u == NG - 1 else 0
        return FIRST + BODY * (NG * b + u) - short

    def place(b, u, ahead):
        return (b + 1, u + ahead - NG) if u + ahead >= NG else (b, u + ahead)

    def turn_pe(pe, b, u, n, turn, slot):
        kind, ahead, j = turn
        bb, uu = place(b, u, ahead)
        if not isinstance(n, int) or n >= 2:
            pe.wait_ge(turn_free, n - 1)
        out = m.mx[slot]
        if kind == "max":
            h, qt = j // LT, j % LT
            if j == 0:
                pe.wait_ge(m.stack_loaded[uu], 64 * (bb + 1))
            for c in range(NC):
                last = pe.matmul(out[:, c * HALF:(c + 1) * HALF], m.qs[0:SHIFT, uu, h, qt * P:(qt + 1) * P],
                                 m.ks[0:SHIFT, uu, h, c * HALF:(c + 1) * HALF], start=True, stop=True)
                if c == 0:
                    yield
        elif kind == "heads":
            for t in range(4):
                last = pe.transpose(out[:, t * P:(t + 1) * P], m.attn[:, j[0], 4 * j[1] + t, :], m.ident[:, :])
        elif kind == "out":
            for t in range(4):
                last = pe.matmul(out[:, t * P:(t + 1) * P], m.pxnT[j[1]][:, t * P:(t + 1) * P], m.wT[:, 3, :],
                                 start=True, stop=True)
        else:
            pe.wait_ge(av_kept, 2 * (4 * bb + uu) + 3)
            for qt in range(LT):
                last = pe.transpose(out[:, qt * P:(qt + 1) * P],
                                    m.avs[:, qt // 4, (qt % 4) * P:(qt % 4 + 1) * P], m.ident[:, :])
        last.then_inc(turn_full, 1)

    def turn_dve(dve, b, u, n, turn, slot):
        kind, ahead, j = turn
        bb, uu = place(b, u, ahead)
        g = 4 * bb + uu
        if kind == "shift":
            dve.wait_ge(shift_made, g + 1)
            if not (isinstance(g, int) and g == 0):
                pb, pu = (bb, uu - 1) if uu else (bb - 1, NG - 1)
                dve.wait_ge(shift_loaded[pu], SHIFT_LOADED * (pb + 1))
            dve.transpose(m.m3T[:, :], m.m3[:, :]).then_inc(shift_turned, 1)
            return
        dve.wait_ge(turn_full, n + 1)
        src = m.mx[slot]
        if kind == "max":
            dve.tensor_reduce(m.maxima[:, uu % 2, j:j + 1], src[:, :], AX.X, ALU.max).then_inc(turn_free, 1)
        elif kind == "heads":
            dve.tensor_copy(m.pxnT[j[1]][:, :], src[:, 0:HALF]).then_inc(turn_free, 1)
        elif kind == "out":
            xs = m.x[:, j[0], 4 * j[1]:4 * j[1] + 4, :]
            dve.tensor_tensor(xs, src[:, 0:HALF].rearrange("p (t d) -> p t d", d=D), xs, ALU.add).then_inc(turn_free, 1)
            dve.wait_ge(turn_free, n + 1)
            chunk_stats(dve, m, *j)
        else:
            t = src[:, :].rearrange("p (q h r) -> p q h r", h=GH, r=32)
            dve.wait_ge(turn_free, n)
            dve.reciprocal(m.recip[:, :, :], t[:, :, :, DH]).then_inc(recip_done, 1)
            dve.wait_ge(recip_done, g + 1)
            o = m.attn[:, bb, :, uu * GH * DH:(uu + 1) * GH * DH].rearrange("p q (h d) -> p q h d", d=DH)
            dve.tensor_tensor(o, t[:, :, :, 0:DH], m.recip[:, :, :].unsqueeze(3).to_broadcast([P, LT, GH, DH]),
                              ALU.mult).then_inc(turn_free, 1)

    def score_bank(b, u, s, c, h):
        n = CH * (s - WIDE_FROM) + GH * c + h
        if not (isinstance(b, int) and (b, u) == (B - 1, NG - 1)) or n < 0:
            return m.st[h % 2][:, :], 2
        banks = [m.st[0][:, :], m.st[1][:, :]] + [m.mx[0][:, j * HALF:(j + 1) * HALF] for j in range(2)]
        return banks[n % 4], (2 if n < 2 else None if n < 4 else 4)

    def scores(pe, b, u, s, c, h):
        k = CH * (LT * (4 * b + u) + s) + GH * c + h
        bank, before = score_bank(b, u, s, c, h)
        if before is None:
            pe.wait_ge(turn_free, first_turn(B - 1, NG - 1))
        elif not isinstance(k, int) or k >= 2:
            pe.wait_ge(exp_done, k - before + 1)
        if s == 0 and c == 0 and h == 0:
            pe.wait_ge(shift_loaded[u], SHIFT_LOADED * (b + 1))
        pe.matmul(bank, m.ks[0:KROWS, u, h, s * P:(s + 1) * P], m.qs[0:KROWS, u, h, c * HALF:(c + 1) * HALF],
                  start=True, stop=True).then_inc(score_full, 1)

    def product(pe, b, u, s, c):
        g = 4 * b + u
        if s == 0 and c == 0:
            pe.wait_ge(v_ready, g + 1)
            pe.wait_ge(av_kept, 2 * g + 1)
        pe.wait_ge(exp_done, CH * (LT * g + s) + GH * (c + 1))
        for h in range(GH):
            last = pe.matmul(m.av[c][32 * h:32 * h + 32, :], m.vgroup[:, u % 2, s, h, :],
                             m.probs[:, s % 2, h, c * HALF:(c + 1) * HALF], start=(s == 0), stop=(s == LT - 1))
        last.then_inc(pv_done, 1)

    def position_pe(pe, b, u, pos, turns, n, slot, has_next):
        makers = [turn_pe(pe, b, u, n + k, t, (slot + k) % 2) for k, t in enumerate(own_turns(turns))]
        for c in range(NC):
            for part, chunk in ROUTES.get((pos, c), []) if not has_next else []:
                if part == "turn":
                    rt.turn(pe, chunk, route_bank)
                elif part == "project":
                    rt.project(pe, chunk)
                else:
                    rt.sum_choices(pe, 0)
            for what in ("S0", "S1", "V", "S2", "M", "S3", "M", "M", "M"):
                if what == "V":
                    if pos > 0 and (pos <= LT or has_next):
                        product(pe, *step_of(b, u, pos - 1), c)
                elif what[0] == "S":
                    if pos < LT or has_next:
                        scores(pe, *step_of(b, u, pos), c, int(what[1]))
                elif makers:
                    if next(makers[0], "end") == "end":
                        makers.pop(0)
        for t in makers:
            for _ in t:
                pass

    def step_of(b, u, pos):
        return (b, u, pos) if pos < LT else (*place(b, u, 1), pos - LT)

    def body_pe(pe, b, u, has_next, has_second):
        k = 0
        for pos, turns in schedule(has_next, has_second).items():
            position_pe(pe, b, u, pos, turns, first_turn(b, u) + k, first_turn(0, u) + k if has_next else 0, has_next)
            k += len(own_turns(turns))

    def body_act(act, b, u, has_next):
        for pos in BODY_POS:
            for c in range(NC):
                if pos < LT or has_next:
                    exps(act, *step_of(b, u, pos), c, range(2))
                if pos == LT:
                    act.wait_ge(pv_done, 2 * (LT * (4 * b + u) + LT - 1) + c + 2)
                    act.activation(m.avs[:, c, :], m.av[c][:, :], ACT.Copy).then_inc(av_kept, 1)
                if pos < LT or has_next:
                    exps(act, *step_of(b, u, pos), c, range(2, GH))
        if not has_next:
            rt.exps(act, 0)

    def exps(act, b, u, s, c, heads):
        for h in heads:
            act.wait_ge(score_full, CH * (LT * (4 * b + u) + s) + GH * c + h + 1)
            act.activation(m.probs[:, s % 2, h, c * HALF:(c + 1) * HALF], score_bank(b, u, s, c, h)[0], ACT.Exp,
                           scale=SCALE).then_inc(exp_done, 1)

    def first_turns():
        alone = [("max", 0, j) for j in range(ITEMS)] + [("max", 1, j) for j in range(2)] + [("shift", 0, 0)]
        alone += [("max", 1, j) for j in range(2, EARLY // 2)]
        ahead = [("max", 1, j) for j in range(EARLY // 2, EARLY)]
        return [alone, ahead[:EARLY // 4], ahead[EARLY // 4:]]

    def bodies(f):
        def run(eng):
            with eng.Fori(0, B - 1) as b:
                for u in range(NG):
                    f(eng, b, u, True, True)
            for u in range(NG):
                f(eng, B - 1, u, u < NG - 1, u < NG - 2)
        return run

    def load_shift(sp, b, u):
        sp.wait_ge(shift_turned, NG * b + u + 1)
        g = NG * b + u
        sp.dma_start(m.shift_rows[b, u, :, :, :, :].rearrange("a c p r -> (a c) p r"),
                     m.m3T[:, :].rearrange("k (p r) -> k p r", p=3)).then_inc(shift_stored, 16)
        sp.wait_ge(shift_stored, 16 * (g + 1))
        for part in range(3):
            sp.dma_start(m.qs[SHIFT + part:SHIFT + part + 1, u, :, :].rearrange("o h (q a r) -> o (h q) a r", q=LT, a=4),
                         m.shift_rows[b, u, :, :, part:part + 1, :].rearrange("a c o r -> o c a r")).then_inc(shift_loaded[u], 16)

    def last_maximum(b, u):
        if isinstance(b, int) and b == 0 and u == 0:
            return ITEMS - 1
        pb, pu = (b, u - 1) if u else (b - 1, NG - 1)
        return first_turn(pb, pu) + 4 * LATE_POS - 1

    with nc.Block() as block:
        @block.tensor
        def _(pe):
            pe.sem_inc(pv_done, 1)
            alone, *ahead = first_turns()
            for n, turn in enumerate(own_turns(alone)):
                for _ in turn_pe(pe, 0, 0, n, turn, n % 2):
                    pass
            n = len(own_turns(alone))
            for pos, turns in enumerate(ahead):
                position_pe(pe, 0, 0, pos, turns, n, n, True)
                n += len(own_turns(turns))
            bodies(body_pe)(pe)

        @block.vector
        def _(dve):
            n = 0
            for turn in [t for part in first_turns() for t in part]:
                turn_dve(dve, 0, 0, n, turn, n % 2)
                n += len(own_turns([turn]))

            def body(eng, b, u, has_next, has_second):
                k = 0
                if not has_next:
                    for bb in range(B - 1):
                        layer_norm_step(eng, m, rt, bb)
                    for bb in range(B - 1):
                        rt.normalise(eng, bb)
                    for c in range(NC * (B - 1)):
                        rt.keep(eng.tensor_copy, eng, c, route_bank)
                    rt.choose(eng, 0, NC * (B - 1))
                    rt.divide(eng, 0)
                for turn in [t for x in schedule(has_next, has_second).values() for t in x]:
                    turn_dve(eng, b, u, first_turn(b, u) + k, turn, (first_turn(0, u) + k) % 2 if has_next else 0)
                    k += len(own_turns([turn]))
            bodies(body)(dve)

        @block.scalar
        def _(act):
            finish_act(act)
            act.sem_inc(av_kept, 1)
            for s in range(2):
                for c in range(NC):
                    exps(act, 0, 0, s, c, range(GH))
            bodies(lambda eng, b, u, has_next, _: body_act(eng, b, u, has_next))(act)

        @block.gpsimd
        def _(pool):
            def copy_v(b, u):
                pool.tensor_copy(m.vgroup[:, u % 2, :, :, 0:DH],
                                 m.v[:, b, :, u * GH * DH:(u + 1) * GH * DH].rearrange("p t (h d) -> p t h d", d=DH))\
                    .then_inc(v_ready, 1)
            def split_maxima(b, u):
                g = NG * b + u
                mx = m.maxima[:, u % 2, :]
                parts = [m.m3[:, i * ITEMS:(i + 1) * ITEMS] for i in range(3)]
                pool.wait_ge(turn_free, last_maximum(b, u) + 1)
                if not (isinstance(g, int) and g == 0):
                    pool.wait_ge(shift_turned, g)
                pool.tensor_tensor(m.mneg[:, :], m.zeros[:, 0:ITEMS], mx, ALU.subtract).then_inc(split, 1)
                pool.wait_ge(split, 4 * g + 1)
                pool.tensor_tensor(parts[0], m.zeros[:, 0:ITEMS], mx, ALU.subtract).then_inc(split, 1)
                pool.wait_ge(split, 4 * g + 2)
                pool.tensor_tensor(m.mrest[:, :], m.mneg[:, :], parts[0], ALU.subtract).then_inc(split, 1)
                pool.wait_ge(split, 4 * g + 3)
                pool.tensor_tensor(parts[1], m.zeros[:, 0:ITEMS], m.mrest[:, :], ALU.add).then_inc(split, 1)
                pool.wait_ge(split, 4 * g + 4)
                pool.tensor_tensor(parts[2], m.mrest[:, :], parts[1], ALU.subtract).then_inc(shift_made, 1)
            finish_pool(pool)
            copy_v(0, 0)
            split_maxima(0, 0)

            def body(eng, b, u, has_next, _):
                if has_next:
                    eng.wait_ge(pv_done, 2 * LT * (4 * b + u) + 1)
                    copy_v(*place(b, u, 1))
                    split_maxima(*place(b, u, 1))
                else:
                    for bb in range(B - 1):
                        layer_norm_roots(eng, m, rt, bb)
            bodies(body)(pool)

        @block.sync
        def _(sp):
            finish_sp(sp)
            load_shift(sp, 0, 0)

            def body(eng, b, u, has_next, has_second):
                if has_second:
                    load_stack(eng, m, *place(b, u, 2))
                if has_next:
                    load_shift(eng, *place(b, u, 1))
            bodies(body)(sp)
            for s in range(SLOTS):
                sp.wait_ge(shift_loaded[s], SHIFT_LOADED * B)


def program(nc, x, w_qkv, w_out, router, w1, b1, w2, b2, cos, sin, consts, out):
    with ExitStack() as ctx:
        m = Memory(nc, ctx)
        q_parts = nc.dram_tensor("q_parts", (B, H, STACK, L), BF16, kind="Internal").ap()
        k_parts = nc.dram_tensor("k_parts", (B, H, 3 * DH, L), BF16, kind="Internal").ap()

        m.shift_rows = nc.dram_tensor("shift_rows", (B, NG, 4, GH * LT, 3, 32), BF16, kind="Internal").ap()

        def q_store(b, part, copy):
            r = (3 * part + copy) * DH
            return q_parts[b, :, r:r + DH, :]

        def k_store(b, part):
            return k_parts[b, :, part * DH:(part + 1) * DH, :]

        def stack_q(b, u):
            return q_parts[b, u * GH:(u + 1) * GH, :, :].rearrange("h r t -> r h t")

        def stack_k(b, u):
            return k_parts[b, u * GH:(u + 1) * GH, :, :].rearrange("h r t -> r h t")

        m.q_store, m.k_store, m.stack_q, m.stack_k = q_store, k_store, stack_q, stack_k
        m.x = m.sb("x_tokens", [P, B, LT, D])
        m.ident = m.sb("identity", [P, P])
        m.wT = m.sb("w_transposed", [P, 4, D])
        m.wrT = m.sb("w_rotated", [P, 2, D])
        m.cos = m.sb("rope_cos", [P, L])
        m.sin = m.sb("rope_sin", [P, L])
        m.stats = m.sb("ln_stats", [P, TILES, 6])
        m.ln_tmp = m.sb("ln_steps", [P, 4, TILES])
        m.mean = m.sb("ln_mean", [P, TILES])
        m.shift = m.sb("ln_shift", [P, TILES])
        m.veps = m.sb("ln_var_eps", [P, TILES])
        m.rstd = m.sb("ln_rstd", [P, TILES])
        m.minus_half = m.sb("minus_half", [P, TILES])
        scratch = m.sb("scratch", [P, 4 * RING * D])
        m.pxnT = [scratch[:, i * HALF:(i + 1) * HALF] for i in range(2)]
        m.avs = scratch[:, L:2 * L].rearrange("p (c t) -> p c t", c=NC)
        m.xblk, m.yblk = (scratch[:, n * 2 * RING * D:(n + 1) * 2 * RING * D].rearrange("p (s r d) -> p s r d", s=2, d=D)
                          for n in range(2))
        m.attn = m.sb("attn_tokens", [P, B, LT, D])
        m.qs = m.sb("q_stacks", [KROWS, SLOTS, GH, L], BF16)
        m.ks = m.sb("k_stacks", [KROWS, SLOTS, GH, L], BF16)
        m.vgroup = m.sb("v_group", [P, 2, LT, GH, 32])
        m.maxima = m.sb("maxima", [P, 2, GH * LT])
        m.mneg = m.sb("maxima_negated", [P, GH * LT])
        m.zeros = m.sb("zeros", [P, D])
        m.mrest = m.sb("maxima_rest", [P, GH * LT])
        m.m3 = m.sb("maxima_parts", [P, 3 * GH * LT], BF16)
        m.m3T = m.sb("maxima_rows", [P, 3 * GH * LT], BF16)
        m.recip = m.sb("sum_recips", [P, LT, GH])
        m.st = [m.ps(f"scores{i}", [P, HALF]) for i in range(2)]
        m.mx = [m.ps(f"turn{i}", [P, L]) for i in range(2)]
        m.av = [m.ps(f"av{i}", [P, HALF]) for i in range(2)]
        routing = m.sb("routing", [P, 5 * TILES * E])
        shared = m.sb("shared", [P, SHARED])
        at = [0]

        def take(n):
            at[0] += n
            assert at[0] <= SHARED
            return shared[:, at[0] - n:at[0]]
        m.probs = take(2 * GH * L).rearrange("p (s h t) -> p s h t", s=2, h=GH)
        m.v = take(B * LT * D).rearrange("p (b i d) -> p b i d", b=B, i=LT)
        m.parts = [a.bitcast(BF16).rearrange("p (n i t) -> p n i t", n=2, i=3)
                   for a in (take(3 * L), m.attn[:, 1:4, :, :].rearrange("p b i d -> p (b i d)"))]
        m.xn = [m.probs[:, 0, 0, :].rearrange("p (i d) -> p i d", d=D), m.attn[:, 0, :, :]]
        halves = lambda a: a.rearrange("p (n t) -> p n t", n=2)
        m.tcos = [halves(m.probs[:, i, 1, :]) for i in range(2)]
        m.tsin = [halves(m.probs[:, i, 2, :]) for i in range(2)]
        m.roped = [halves(m.probs[:, i, 3, :]) for i in range(2)]
        m.rest = [halves(m.probs[:, 1, 0, :]), halves(routing[:, 0:L])]
        at[0] = 0
        m.wx = take(E * WX).rearrange("p (e w) -> p e w", e=E)
        m.hid = take(RING * F).rearrange("p (r c t) -> p r c t", r=RING, c=FC)
        m.fxnT = shared[:, SHARED - 3 * L:SHARED - 3 * L + 4 * HALF].rearrange("p (c t) -> p c t", c=4)
        m.wblk = take(RING * WX).rearrange("p (r w) -> p r w", r=RING)
        m.xT = take(RING * P).rearrange("p (r d) -> p r d", r=RING)
        m.rows = m.attn
        m.router = m.sb("router", [P, E])
        m.b1_rows = m.sb("b1_rows", [E * FC, P])
        m.rt = [routing[:, i * TILES * E:(i + 1) * TILES * E].rearrange("p (t e) -> p t e", e=E) for i in range(5)]
        m.choice = m.sb("choice", [P, TILES, E], BF16)
        m.ones = m.sb("ones", [P, TILES * E])
        m.ones_bf = m.sb("ones_bf", [P, P], BF16)
        m.upper = m.sb("upper_triangle", [P, P], BF16)
        m.consts = m.sb("consts", [P, E + HT + HB])
        m.tmax = m.sb("logit_max", [P, TILES])
        m.tfirst = m.sb("first_choice", [P, TILES])
        m.per_e = m.sb("per_expert", [P, 2, 5, E])
        m.slot_f = m.sb("slots", [P, TILES])
        m.slot_i = m.sb("slot_indices", [P, TILES], mybir.dt.uint32)
        m.block_cmp = routing[0:1, 4 * TILES * E:4 * TILES * E + HB * E].rearrange("o (n e) -> o n e", e=E)
        m.block_f = m.sb("block_count", [1, BLOCKS])
        m.block_e = m.sb("block_experts", [1, ROUNDS // 2, 2 * RING], mybir.dt.int32)
        m.psum_e = m.sb("exp_sums", [P, TILES])
        m.half_p = m.sb("half_probability", [P, TILES])
        m.slots_in, m.slots_out = ([nc.dram_tensor(f"slots_{way}{h}", (HB, P, D), FP32, kind="Internal").ap() for h in range(2)]
                                   for way in ("in", "out"))
        m.x_loaded = [m.sem(f"x{b}_loaded") for b in range(B)]
        m.router_loaded, m.bias_loaded = m.sem("router_loaded"), m.sem("bias_loaded")
        m.weights_loaded = m.sem("weights_loaded")
        m.consts_loaded, m.tables_loaded = m.sem("consts_loaded"), m.sem("tables_loaded")
        m.slots_cleared, m.rows_set = m.sem("slots_cleared"), m.sem("stack_rows_set")
        m.out_stored = m.sem("out_stored")

        m.parts_stored = [m.sem(f"parts{i}_stored") for i in range(2)]
        m.stack_loaded = [m.sem(f"stack{s}_loaded") for s in range(SLOTS)]
        m.stats_done, m.stats_count = m.sem("stats_done"), [0]
        routers = [Router(m, f"ffn{n}") for n in (1, 2)]
        norm = LayerNorm(m)
        setup_stage(nc, m, x, router, b1, consts)
        last_outputs = ffn_stage(nc, m, "ffn1", routers[0], w1, w2, b2, attention=(w_qkv, w_out, cos, sin), norm=norm)
        last_parts = project_stage(nc, m, norm, *last_outputs)
        attention_stage(nc, m, routers[1], last_parts)
        ffn_stage(nc, m, "ffn2", routers[1], w1, w2, b2, out=out)


def rope_tables():
    import numpy as np
    half = DH // 2
    inv = (np.float32(1.0) / np.power(np.float32(10000.0), np.arange(half, dtype=np.float32) / np.float32(half))).astype(np.float32)
    ang = (np.arange(L, dtype=np.float32)[:, None] * inv[None, :]).astype(np.float32)
    cos = np.concatenate([np.cos(ang), np.cos(ang)], axis=-1).astype(np.float32).T
    sin = np.concatenate([np.sin(ang), np.sin(ang)], axis=-1).astype(np.float32).T
    return np.tile(cos, (H, 1)), np.tile(sin, (H, 1))


def shape_constants():
    import numpy as np
    row = np.concatenate([np.arange(E, 0, -1), np.arange(HT) * P, np.arange(HB)]).astype(np.float32)
    return np.tile(row, (P, 1))


_INS = ["L0_attn_x", "L0_attn_w_qkv", "L0_attn_w_out", "L0_ffn_router_w", "L0_ffn_w1", "L0_ffn_b1", "L0_ffn_w2", "L0_ffn_b2"]


def kernel(**inputs):
    import numpy as _np
    import concourse.bacc as _bacc
    from concourse import mybir as _mybir
    from concourse.bass_utils import run_bass_kernel_spmd as _run

    nc = _bacc.Bacc("TRN2", target_bir_lowering=False, num_devices=1)
    arrays, args = {}, []
    cos, sin = rope_tables()
    given = [(n, inputs[n]) for n in _INS] + [("rope_cos", cos), ("rope_sin", sin), ("shape_constants", shape_constants())]
    for name, a in given:
        a = _np.ascontiguousarray(a)
        arrays[f"in_{name}_dram"] = a
        args.append(nc.dram_tensor(f"in_{name}_dram", a.shape, _mybir.dt.from_np(a.dtype), kind="ExternalInput").ap())
    out = nc.dram_tensor("out_0_dram", (B, L, D), FP32, kind="ExternalOutput").ap()
    program(nc, *args, out)
    r = _run(nc, [arrays], core_ids=[0])
    return r.results[0]["out_0_dram"]
```
